# Optimizing a Trainium2 kernel written in Bass

```python
import numpy as np
import jax
import jax.numpy as jnp

def _softmax(x, axis=-1):
    return jax.nn.softmax(x, axis=axis)

def _gelu(x):
    return jax.nn.gelu(x, approximate=True)

def _silu(x):
    return jax.nn.silu(x)

def _sigmoid(x):
    return jax.nn.sigmoid(x)

def _layernorm(x, axis=-1, eps=1e-05):
    m = jnp.mean(x, axis=axis, keepdims=True)
    v = jnp.var(x, axis=axis, keepdims=True)
    return (x - m) / jnp.sqrt(v + eps)

def _scatter_add(tgt, idx, src, axis=0):
    return tgt.at[idx].add(src)

def _segment_sum(src, seg, n):
    return jax.ops.segment_sum(src, seg, n)
kernel_name = 'mk_seq_preln_d1_jaxref_r8_2949f0'

def setup_inputs(seed: int=0):
    np.random.seed(seed)
    _w = jnp.asarray

    def _L0_attn_setup():
        import jax, jax.numpy as jnp
        import numpy as np
        N_HEAD = 16
        key = jax.random.key(seed)
        k1, k2, k3 = jax.random.split(key, 3)
        B, T, C = (2, 256, 256)
        x = jax.random.normal(k1, (B, T, C), dtype=jnp.float32)
        w_attn = jax.random.normal(k2, (C, 3 * C), dtype=jnp.float32) * (1.0 / np.sqrt(C))
        w_proj = jax.random.normal(k3, (C, C), dtype=jnp.float32) * (1.0 / np.sqrt(C))
        return {'x': x, 'w_attn': w_attn, 'w_proj': w_proj}
    _L0_attn_in = _L0_attn_setup()

    def _L0_ffn_setup():
        import jax, jax.numpy as jnp
        import numpy as np
        B, S, D = (2, 256, 256)
        E, I, TOPK = (64, 96, 8)
        M = B * S
        CAP = 2 * (M * TOPK) // E

        def _moe(x, router_weight, gate_proj, up_proj, down_proj):
            b, s, d = x.shape
            xf = x.reshape(-1, d)
            m = xf.shape[0]
            logits = xf @ router_weight
            probs = jax.nn.softmax(logits.astype(jnp.float32), axis=-1)
            topw, topi = jax.lax.top_k(probs, TOPK)
            topw = topw / topw.sum(axis=-1, keepdims=True)
            flat_e = topi.reshape(-1)
            flat_w = topw.reshape(-1).astype(x.dtype)
            order = jnp.argsort(flat_e)
            se = flat_e[order]
            tok = order // TOPK
            counts = jax.ops.segment_sum(jnp.ones_like(flat_e), flat_e, num_segments=E)
            starts = jnp.cumsum(counts) - counts
            pos = jnp.arange(m * TOPK) - starts[se]
            valid = pos < CAP
            posc = jnp.minimum(pos, CAP - 1)
            xe = jnp.zeros((E, CAP, d), x.dtype).at[se, pos].set(xf[tok], mode='drop')
            h = jax.nn.silu(jnp.einsum('ecd,edi->eci', xe, gate_proj)) * jnp.einsum('ecd,edi->eci', xe, up_proj)
            ye = jnp.einsum('eci,eid->ecd', h, down_proj)
            contrib = jnp.where(valid[:, None], ye[se, posc], 0.0) * flat_w[order][:, None]
            out = jnp.zeros((m, d), x.dtype).at[tok].add(contrib)
            return out.reshape(b, s, d)
        key = jax.random.key(seed)
        k0, k1, k2, k3, k4 = jax.random.split(key, 5)
        return {'x': jax.random.normal(k0, (B, S, D), jnp.float32), 'router_weight': jax.random.normal(k1, (D, E), jnp.float32) * 0.02, 'gate_proj': jax.random.normal(k2, (E, D, I), jnp.float32) * 0.02, 'up_proj': jax.random.normal(k3, (E, D, I), jnp.float32) * 0.02, 'down_proj': jax.random.normal(k4, (E, I, D), jnp.float32) * 0.02}
    _L0_ffn_in = _L0_ffn_setup()
    _d = {'L0_attn_x': _L0_attn_in['x'], 'L0_attn_w_attn': _L0_attn_in['w_attn'], 'L0_attn_w_proj': _L0_attn_in['w_proj'], 'L0_ffn_router_weight': _L0_ffn_in['router_weight'], 'L0_ffn_gate_proj': _L0_ffn_in['gate_proj'], 'L0_ffn_up_proj': _L0_ffn_in['up_proj'], 'L0_ffn_down_proj': _L0_ffn_in['down_proj']}
    _x0 = _d['L0_attn_x']
    _d['L0_attn_x'] = jax.random.normal(jax.random.fold_in(jax.random.key(seed), 1), (8, 512, 256), dtype=_x0.dtype)
    del _x0
    return _d

def reference(L0_attn_x, L0_attn_w_attn, L0_attn_w_proj, L0_ffn_router_weight, L0_ffn_gate_proj, L0_ffn_up_proj, L0_ffn_down_proj):

    def _L0_attn_ref(x, w_attn, w_proj):
        import jax, jax.numpy as jnp
        import numpy as np
        N_HEAD = 16
        B, T, C = x.shape
        H = N_HEAD
        D = C // H
        qkv = x @ w_attn
        q, k, v = jnp.split(qkv, 3, axis=-1)
        q = q.reshape(B, T, H, D).transpose(0, 2, 1, 3)
        k = k.reshape(B, T, H, D).transpose(0, 2, 1, 3)
        v = v.reshape(B, T, H, D).transpose(0, 2, 1, 3)
        scale = 1.0 / np.sqrt(D).astype(np.float32)
        att = jnp.einsum('bhqd,bhkd->bhqk', q, k) * scale
        causal = jnp.tril(jnp.ones((T, T), dtype=bool))
        att = jnp.where(causal[None, None, :, :], att, jnp.float32(-jnp.inf))
        att = jax.nn.softmax(att, axis=-1)
        y = jnp.einsum('bhqk,bhkd->bhqd', att, v)
        y = y.transpose(0, 2, 1, 3).reshape(B, T, C)
        return y @ w_proj

    def _L0_ffn_ref(x, router_weight, gate_proj, up_proj, down_proj):
        import jax, jax.numpy as jnp
        import numpy as np
        B, S, D = (2, 256, 256)
        E, I, TOPK = (64, 96, 8)
        M = B * S
        CAP = 2 * (M * TOPK) // E

        def _moe(x, router_weight, gate_proj, up_proj, down_proj):
            b, s, d = x.shape
            xf = x.reshape(-1, d)
            m = xf.shape[0]
            logits = xf @ router_weight
            probs = jax.nn.softmax(logits.astype(jnp.float32), axis=-1)
            topw, topi = jax.lax.top_k(probs, TOPK)
            topw = topw / topw.sum(axis=-1, keepdims=True)
            flat_e = topi.reshape(-1)
            flat_w = topw.reshape(-1).astype(x.dtype)
            order = jnp.argsort(flat_e)
            se = flat_e[order]
            tok = order // TOPK
            counts = jax.ops.segment_sum(jnp.ones_like(flat_e), flat_e, num_segments=E)
            starts = jnp.cumsum(counts) - counts
            pos = jnp.arange(m * TOPK) - starts[se]
            valid = pos < CAP
            posc = jnp.minimum(pos, CAP - 1)
            xe = jnp.zeros((E, CAP, d), x.dtype).at[se, pos].set(xf[tok], mode='drop')
            h = jax.nn.silu(jnp.einsum('ecd,edi->eci', xe, gate_proj)) * jnp.einsum('ecd,edi->eci', xe, up_proj)
            ye = jnp.einsum('eci,eid->ecd', h, down_proj)
            contrib = jnp.where(valid[:, None], ye[se, posc], 0.0) * flat_w[order][:, None]
            out = jnp.zeros((m, d), x.dtype).at[tok].add(contrib)
            return out.reshape(b, s, d)
        return _moe(x, router_weight, gate_proj, up_proj, down_proj)
    x = L0_attn_x
    x = x + _L0_attn_ref(_layernorm(x, axis=-1), L0_attn_w_attn, L0_attn_w_proj)
    x = x + _L0_ffn_ref(_layernorm(x, axis=-1), L0_ffn_router_weight, L0_ffn_gate_proj, L0_ffn_up_proj, L0_ffn_down_proj)
    return x

_drawn_inputs = setup_inputs


def setup_inputs(seed=0):
    import zlib

    import numpy as np

    out = dict(_drawn_inputs(seed))
    spreads = {}
    factors = {'L0_ffn_router_weight': 8.0,
     'L0_ffn_gate_proj': 8.0,
     'L0_ffn_up_proj': 8.0,
     'L0_ffn_down_proj': 8.0}
    for name, (base, spread) in spreads.items():
        noise = np.random.default_rng([zlib.crc32(name.encode()), seed]).standard_normal(out[name].shape)
        drawn = base * np.exp(spread * noise) if base else spread * noise
        out[name] = jnp.asarray(drawn.astype(out[name].dtype))
    for name, factor in factors.items():
        out[name] = (out[name] * factor).astype(out[name].dtype)
    return out
```

```python
from contextlib import ExitStack

import concourse.bass as bass
from concourse import mybir

ALU = mybir.AluOpType
ACT = mybir.ActivationFunctionType
AX = mybir.AxisListType
F32 = mybir.dt.float32
BF16 = mybir.dt.bfloat16
I32 = mybir.dt.int32
U32 = mybir.dt.uint32

P = 128
B = 8
T = 512
C = 256
H = 16
D = 16
E = 64
I = 96
TOPK = 8
CAP = 128
N = B * T
TT = T // P
CC = C // P
GH = 4
NG = H // GH
ROWW = C + E
EPS = 1e-5
SCALE = 0.25
NEG = -1e30
QPART = (0, 0, 0, 1, 1, 2)
KPART = (0, 1, 2, 0, 1, 0)
KROWS = D * len(QPART)
MROWS = KROWS + 3
LAG = 8
FILLS = (((0, 3, 0),), ((0, 2, 0), (0, 0, 384)), ((1, 3, 0),), ((1, 2, 0), (1, 0, 384)), ((0, 1, 0), (1, 1, 256)))
NF = len(FILLS) * H // 2
MAXIMA = 4 * H
ST_AT = {0: 0, 1: 512, 3: 896, 2: 1024}
PW = 1280


def due(eng, sem, per, b, k, apart=None):
    if isinstance(b, int):
        if per * b + k > 0:
            eng.wait_ge(sem, per * b + k)
        return
    eng.wait_ge(sem, b * per + k)
    if apart is not None:
        eng.sem_inc(apart, 1)


def fills_of(slot):
    first = len(FILLS) * (slot // 2)
    return range(first, first + 2) if slot % 2 == 0 else range(first + 2, first + 5)


def maxima_by(n):
    pair, f = divmod(n, len(FILLS))
    return 8 * pair + sum(len(x) for x in FILLS[:f + 1])


def attention(nc, x, w_attn, w_proj, w_router, parts_d, acc0, acc1, table_d, maskT_d):
    x_v = x.rearrange("b (t p) c -> b p t c", p=P)
    acc0_v = acc0[0:N, :].rearrange("(b t p) c -> b p t c", t=TT, p=P)
    table_v = table_d.rearrange("(b t p) c -> b p t c", t=TT, p=P)
    with ExitStack() as ctx:
        def sb(name, shape, dt=F32):
            return ctx.enter_context(nc.sbuf_tensor(name, shape, dt))

        def sem(name):
            return ctx.enter_context(nc.semaphore(name))

        wqkv = sb("wqkv", [P, CC, 3 * C])
        wp = sb("wp", [P, CC, C])
        wr = sb("wr", [P, CC, E])
        ident = sb("ident", [P, P])
        identb = sb("identb", [P, P], BF16)
        causal = sb("causal", [P, T])
        minus_half = sb("minus_half", [P, 2 * TT])
        zeros = sb("zeros", [P, C])
        xa = sb("xa", [P, TT, C])
        xb = sb("xb", [P, TT, C])
        xn = sb("xn", [P, TT, C])
        xnT = sb("xnT", [P, CC, T])
        stats1 = sb("stats1", [P, TT, 6])
        mv1 = sb("mv1", [P, TT, 2])
        ve1 = sb("ve1", [P, TT])
        rstd1 = sb("rstd1", [P, TT])
        part = [sb(f"part{n}", [P, 4, T], BF16) for n in range(3)]
        rest = sb("rest", [P, 2, T])
        Qs = [sb(f"Qs{n}", [P, H, T], BF16) for n in range(2)]
        Ks = [sb(f"Ks{n}", [P, H, T], BF16) for n in range(2)]
        Va = [sb(f"Va{n}", [P, TT, H, 2 * D]) for n in range(2)]
        junk = sb("junk", [P, 2 * T], BF16)
        rowmax = sb("rowmax", [P, TT, H])
        nrest = sb("nrest", [P, TT, GH])
        nparts = sb("nparts", [P, TT, 3, GH], BF16)
        npT = sb("npT", [3 * GH, T], BF16)
        pT = sb("pT", [P, 2 * GH, PW])
        oT = sb("oT", [P, NG, T])
        rsum = sb("rsum", [P, TT, H])
        y = sb("y", [P, TT, C])
        yT = sb("yT", [P, CC, T])
        x2 = sb("x2", [P, TT, C])
        stats2 = sb("stats2", [P, TT, 6])
        mv2 = sb("mv2", [P, TT, 2])
        ve2 = sb("ve2", [P, TT])
        rstd2 = sb("rstd2", [P, TT])
        row = sb("row", [P, TT, ROWW])
        xn2T = sb("xn2T", [P, CC, T])
        logit = sb("logit", [P, TT, E])
        cut = sb("cut", [P, TT, E])
        top = sb("top", [P, TT, TOPK])
        nmax = sb("nmax", [P, TT])
        chosen = sb("chosen", [P, TT, 2, E], BF16)
        ex = sb("ex", [P, TT, E])
        wts = sb("wts", [P, TT, E])
        wsum = sb("wsum", [P, TT])
        winv = sb("winv", [P, TT])
        chosenT = sb("chosenT", [P, T], BF16)

        ps_max = [ctx.enter_context(nc.psum_tensor(f"ps_max{n}", [P, T], F32)) for n in range(2)]
        ps_exp = ctx.enter_context(nc.psum_tensor("ps_exp", [P, 1536], F32))
        ps_pv = ctx.enter_context(nc.psum_tensor("ps_pv", [P, T], F32))
        ps_jobs = [ctx.enter_context(nc.psum_tensor(f"ps_job{n}", [P, T], F32)) for n in range(2)]

        s_w = sem("weights_in")
        s_passed = sem("passed")
        s_zero = sem("zeros_ready")
        s_const = sem("consts_ready")
        s_id0 = sem("const_fill")
        s_ones = sem("ones_ready")
        s_vones = sem("v_ones_ready")
        s_acc = sem("accumulators_zeroed")
        s_xa = sem("xa_in")
        s_xb = sem("xb_in")
        s_st1 = sem("stats1_ready")
        s_mv1 = sem("mv1_ready")
        s_ve1 = sem("ve1_ready")
        s_rs1 = sem("rstd1_ready")
        s_xn = sem("xn_ready")
        s_xnT_mm = sem("xnT_in_psum")
        s_xnT = sem("xnT_ready")
        s_qk_mm = sem("qk_in_psum")
        s_p1 = sem("part1_ready")
        s_rest = sem("rest_ready")
        s_p2 = sem("part2_ready")
        s_p3 = sem("part3_ready")
        s_pst = sem("parts_stored")
        s_stk = [sem(f"stacks_in{n}") for n in range(2)]
        s_v_mm = sem("v_in_psum")
        s_v = sem("v_ready")
        s_s = sem("scores_in_psum")
        s_max = sem("rowmax_ready")
        s_np = sem("negmax_steps")
        s_np_mm = sem("negmaxT_in_psum")
        s_npT = sem("negmaxT_ready")
        s_nrow = [sem(f"negmax_rows_in{g}") for g in range(NG)]
        s_sT = sem("scoresT_in_psum")
        s_exp = sem("exp_ready")
        s_msk = sem("probs_masked")
        s_pv = sem("pv_in_psum")
        s_oT = sem("oT_ready")
        s_o_mm = sem("o_in_psum")
        s_rsum = sem("rowsum_inverse_ready")
        s_y = sem("y_ready")
        s_yT_mm = sem("yT_in_psum")
        s_yT = sem("yT_ready")
        s_pr_mm = sem("proj_in_psum")
        s_x2 = sem("x2_ready")
        s_x2st = sem("x2_stored")
        s_st2 = sem("stats2_ready")
        s_mv2 = sem("mv2_ready")
        s_ve2 = sem("ve2_ready")
        s_rs2 = sem("rstd2_ready")
        s_row = sem("xn2_ready")
        s_x2T_mm = sem("xn2T_in_psum")
        s_x2T = sem("xn2T_ready")
        s_lg_mm = sem("logits_in_psum")
        s_lg = sem("logits_ready")
        s_top = sem("topk_steps")
        s_ex = sem("router_exp_ready")
        s_rowst = sem("table_stored")
        s_ch_mm = sem("chosenT_in_psum")
        s_ch = sem("chosenT_ready")
        s_chst = sem("chosenT_stored")

        JOBS = [
            (0, "yT", 0, -2), (1, "npT", 3, -1), (1, "yT", 1, -2), (2, "proj", 0, -2), (2, "xnT", 0, 1),
            (3, "proj", 1, -2), (3, "xnT", 1, 1), (4, "npT", 0, 0), (4, "qk", 0, 1), (5, "qk", 1, 1),
            (6, "qk", 2, 1), (7, "qk", 3, 1), (8, "npT", 1, 0), (8, "x2T", 0, -2), (9, "x2T", 1, -2),
            (10, "lg", 0, -2), (12, "npT", 2, 0), (12, "v", 0, 1), (13, "v", 1, 1), (13, "ch", 0, -2),
            (14, "o", 0, -1), (14, "o", 1, -1), (15, "o", 2, -1), (15, "o", 3, -1),
        ]
        TAKEN = {"xnT": (s_xnT, 2), "qk": (s_rest, 4), "v": (s_v, 2), "npT": (s_npT, 4), "o": (s_y, 4),
                 "yT": (s_yT, 2), "proj": (s_x2, 2), "x2T": (s_x2T, 2), "lg": (s_lg, 1), "ch": (s_ch, 1)}

        BANK = {(name, k): n % 2 for n, (_, name, k, _) in enumerate(JOBS)}

        def jobs(rep, slot=None):
            return [j for j in JOBS if 0 <= rep + j[3] < B and slot in (None, j[0])]

        def walk(eng, body):
            for i in range(-1, 3):
                body(i, i)
            with eng.Fori(3, B - 2, 2) as i:
                body(i, 3)
                body(i + 1, 4)
            for i in range(B - 1, B + 2):
                body(i, i)

        block = ctx.enter_context(nc.Block())

        @block.sync
        def _(sp):
            def body(i, rep):
                on = lambda off: 0 <= rep + off < B

                def negmax_rows(b, par, g):
                    due(sp, s_npT, NG, b, g + 1)
                    for n in range(3):
                        sp.dma_start(Qs[par][KROWS + n:KROWS + n + 1, GH * g:GH * g + GH, :],
                                     npT[GH * n:GH * n + GH, :]).then_inc(s_nrow[g], 16)

                if on(1):
                    due(sp, s_xn, TT, i, TT)
                    sp.dma_start(xa[:, :, :], x_v[i + 1]).then_inc(s_xa, 16)
                if on(-1):
                    negmax_rows(i - 1, (rep - 1) % 2, 3)
                if on(-2):
                    due(sp, s_x2, 2, i - 3, 2)
                    sp.dma_start(xb[:, :, :], x_v[i - 2]).then_inc(s_xb, 16)
                if on(0):
                    negmax_rows(i, rep % 2, 0)
                if on(1):
                    due(sp, s_p3, 4, i + 1, 4)
                    for n in range(3):
                        sp.dma_start(parts_d[i + 1, n].rearrange("(g p) t -> p g t", p=P),
                                     part[n][:, :, :]).then_inc(s_pst, 16)
                if on(-2):
                    due(sp, s_x2, 2, i - 2, 2)
                    sp.dma_start(acc0_v[i - 2], x2[:, :, :]).then_inc(s_x2st, 16)
                if on(0):
                    negmax_rows(i, rep % 2, 1)
                if on(1):
                    due(sp, s_pst, 48, i + 1, 48)
                    par = (rep + 1) % 2
                    for half in range(2):
                        if on(-1) and half == 0:
                            due(sp, s_sT, H, i - 1, H)
                        if on(0) and half == 1:
                            due(sp, s_s, NF, i, NF // 2 + 1)
                        h0 = half * H // 2
                        for st, off, which in ((Ks, C, KPART), (Qs, 0, QPART)):
                            for n, m in enumerate(which):
                                src = parts_d[i + 1, m, off:off + C, :].rearrange("(h d) t -> d h t", d=D)
                                sp.dma_start(st[par][D * n:D * n + D, h0:h0 + H // 2, :],
                                             src[:, h0:h0 + H // 2, :]).then_inc(s_stk[half], 16)
                if on(0):
                    negmax_rows(i, rep % 2, 2)
                if isinstance(i, int) and i == 0:
                    sp.wait_ge(s_zero, 1)
                    sp.dma_start(acc0[N:N + P, :], zeros[:, :]).then_inc(s_acc, 16)
                    sp.dma_start(acc1.rearrange("(t p) c -> p t c", p=P),
                                 zeros[:, :].unsqueeze(1).to_broadcast([P, N // P + 1, C])).then_inc(s_acc, 16)
                if on(-2):
                    due(sp, s_top, 15, i - 2, 15)
                    sp.dma_start(table_v[i - 2], row[:, :, :]).then_inc(s_rowst, 16)
                    due(sp, s_ch, 1, i - 2, 1)
                    sp.dma_start(maskT_d[i - 2], chosenT[:, :]).then_inc(s_chst, 16)

            walk(sp, body)
            sp.wait_ge(s_acc, 32)
            sp.wait_ge(s_x2st, 16 * B)
            sp.wait_ge(s_rowst, 16 * B)
            sp.wait_ge(s_chst, 16 * B)

        @block.gpsimd
        def _(pool):
            pool.memset(zeros[:, :], 0.0).then_inc(s_zero, 1)
            for m in (ident, identb, causal):
                pool.memset(m[:, :], 0.0).then_inc(s_id0, 1)
            pool.memset(minus_half[:, :], -0.5).then_inc(s_const, 1)
            pool.wait_ge(s_id0, 3)
            for m in (ident, identb):
                pool.affine_select(out=m[:, :], in_=m[:, :], compare_op=ALU.not_equal, fill=1.0, base=0,
                                   pattern=[[-1, P]], channel_multiplier=1).then_inc(s_const, 1)
            diag = causal[:, T - P:T]
            pool.affine_select(out=diag, in_=diag, compare_op=ALU.is_ge, fill=NEG, base=0,
                               pattern=[[-1, P]], channel_multiplier=1).then_inc(s_const, 1)
            for v in Va:
                pool.memset(v[:, :, :, D:2 * D], 1.0).then_inc(s_vones, 1)
            pool.wait_ge(s_const, 4)

            def rstd(s_mv, s_ve, s_rs, mv, ve, out, b):
                due(pool, s_mv, TT, b, TT, apart=s_passed)
                pool.tensor_scalar(ve[:, :], mv[:, :, 1], EPS, None, ALU.add).then_inc(s_ve, 1)
                due(pool, s_ve, 1, b, 1)
                pool.tensor_tensor(out[:, :], ve[:, :], minus_half[:, 0:TT], ALU.pow).then_inc(s_rs, 1)

            def body(i, rep):
                on = lambda off: 0 <= rep + off < B
                for s in range(H):
                    if s == 0 and on(1):
                        rstd(s_mv1, s_ve1, s_rs1, mv1, ve1, rstd1, i + 1)
                    if on(-1 if s < LAG else 0):
                        b, h = (i - 1 if s < LAG else i), (s + H - LAG) % H
                        due(pool, s_exp, H, b, h + 1, apart=s_passed)
                        three = pT[:, h % (2 * GH), :].rearrange("p (a n) -> p a n", n=P)[:, 0:9:4, :]
                        pool.affine_select(out=three, in_=three, compare_op=ALU.is_ge, fill=0.0, base=0,
                                           pattern=[[0, 3], [1, P]], channel_multiplier=-1).then_inc(s_msk, 1)
                        one = pT[:, h % (2 * GH), ST_AT[3]:ST_AT[3] + P]
                        pool.affine_select(out=one, in_=one, compare_op=ALU.is_ge, fill=0.0, base=0,
                                           pattern=[[1, P]], channel_multiplier=-1).then_inc(s_msk, 1)
                    for _, name, k, off in jobs(rep, s):
                        if name == "qk":
                            due(pool, s_pst, 48, i + off, 0)
                            due(pool, s_p2, 4, i + off, k + 1)
                            pool.tensor_tensor(part[2][:, k, :], rest[:, k % 2, :], part[1][:, k, :],
                                               ALU.subtract).then_inc(s_p3, 1)
                    if s == 5 and on(-2):
                        rstd(s_mv2, s_ve2, s_rs2, mv2, ve2, rstd2, i - 2)

            walk(pool, body)

        @block.scalar
        def _(act):
            act.dma_start(wqkv[:, :, :], w_attn.rearrange("(a p) n -> p a n", p=P)).then_inc(s_w, 16)
            act.dma_start(wp[:, :, :], w_proj.rearrange("(a p) n -> p a n", p=P)).then_inc(s_w, 16)
            act.dma_start(wr[:, :, :], w_router.rearrange("(a p) n -> p a n", p=P)).then_inc(s_w, 16)
            act.wait_ge(s_vones, 2)

            def take(name, k, i, off, rep):
                b = i + off
                ps_job = ps_jobs[BANK[name, k]]
                job_b = ps_job[:, :].bitcast(BF16)
                par = (rep + off) % 2
                if name == "xnT":
                    due(act, s_v_mm, 2, b, 0)
                    due(act, s_xnT_mm, 2, b, k + 1)
                    act.activation(xnT[:, k, :], ps_job[:, :], ACT.Copy).then_inc(s_xnT, 1)
                if name == "qk":
                    due(act, s_pst, 48, b, 0)
                    due(act, s_qk_mm, 4, b, k + 1)
                    act.activation(part[0][:, k, :], ps_job[:, :], ACT.Copy).then_inc(s_p1, 1)
                    due(act, s_rest, 4, b, k + 1)
                    act.activation(part[1][:, k, :], rest[:, k % 2, :], ACT.Copy).then_inc(s_p2, 1)
                if name == "v":
                    due(act, s_pv, NG, b - 2, NG)
                    due(act, s_v_mm, 2, b, k + 1)
                    act.activation(Va[par][:, 2 * k:2 * k + 2, :, 0:D],
                                   ps_job[:, :].rearrange("p (t h d) -> p t h d", t=2, d=D),
                                   ACT.Copy).then_inc(s_v, 1)
                if name == "npT":
                    if k == 0:
                        due(act, s_nrow[NG - 1], 48, b, 0)
                    else:
                        due(act, s_nrow[k - 1], 48, b, 48)
                    due(act, s_np_mm, NG, b, k + 1)
                    act.activation(npT[:, :], job_b[0:3 * GH, 0:T], ACT.Copy).then_inc(s_npT, 1)
                if name == "yT":
                    due(act, s_pr_mm, 2, b, 0)
                    due(act, s_yT_mm, 2, b, k + 1)
                    act.activation(yT[:, k, :], ps_job[:, :], ACT.Copy).then_inc(s_yT, 1)
                if name == "x2T":
                    due(act, s_lg_mm, 1, b, 0)
                    due(act, s_x2T_mm, 2, b, k + 1)
                    act.activation(xn2T[:, k, :], ps_job[:, :], ACT.Copy).then_inc(s_x2T, 1)
                if name == "ch":
                    due(act, s_chst, 16, b, 0)
                    due(act, s_ch_mm, 1, b, 1)
                    act.activation(chosenT[:, :], job_b[:, 0:T], ACT.Copy).then_inc(s_ch, 1)

            def body(i, rep):
                on = lambda off: 0 <= rep + off < B
                for s in range(H):
                    if on(-1 if s < LAG else 0):
                        b, h = (i - 1 if s < LAG else i), (s + H - LAG) % H
                        due(act, s_pv, NG, b, h // GH - 1)
                        due(act, s_sT, H, b, h + 1)
                        act.activation(pT[:, h % (2 * GH), :], ps_exp[:, 0:PW], ACT.Exp,
                                       scale=SCALE).then_inc(s_exp, 1)
                    g = (s + 4) // GH % NG
                    if s % GH == GH - 1 and on(-1 if s < 12 else 0):
                        b = i - 1 if s < 12 else i
                        due(act, s_o_mm, TT, b, 0)
                        due(act, s_pv, NG, b, g + 1)
                        act.activation(oT[:, g, :], ps_pv[:, :], ACT.Copy).then_inc(s_oT, 1)
                    for _, name, k, off in jobs(rep, s):
                        take(name, k, i, off, rep)
                    if s == 11 and on(-2):
                        due(act, s_top, 15, i - 2, 9)
                        for t in range(TT):
                            act.activation(ex[:, t, :], logit[:, t, :], ACT.Exp,
                                           bias=nmax[:, t:t + 1]).then_inc(s_ex, 1)

            walk(act, body)

        @block.tensor
        def _(pe):
            pe.wait_ge(s_const, 4)
            pe.wait_ge(s_w, 48)
            pe.wait_ge(s_ones, 2)
            pe.wait_ge(s_vones, 2)

            def job(name, k, b):
                ps_job = ps_jobs[BANK[name, k]]
                job_b = ps_job[:, :].bitcast(BF16)
                if name == "xnT":
                    due(pe, s_xn, TT, b, TT)
                    for t in range(TT):
                        mm = pe.transpose(ps_job[:, P * t:P * t + P], xn[:, t, P * k:P * k + P], ident[:, :])
                    mm.then_inc(s_xnT_mm, 1)
                if name == "qk":
                    due(pe, s_xnT, 2, b, 2)
                    for a in range(CC):
                        mm = pe.matmul(ps_job[:, :], wqkv[:, a, P * k:P * k + P], xnT[:, a, :],
                                       start=(a == 0), stop=(a == CC - 1))
                    mm.then_inc(s_qk_mm, 1)
                if name == "v":
                    for t in (2 * k, 2 * k + 1):
                        for a in range(CC):
                            mm = pe.matmul(ps_job[:, C * (t % 2):C * (t % 2) + C], xnT[:, a, P * t:P * t + P],
                                           wqkv[:, a, 2 * C:3 * C], start=(a == 0), stop=(a == CC - 1))
                    mm.then_inc(s_v_mm, 1)
                if name == "npT":
                    due(pe, s_np, 4 * NG, b, 4 * k + 4)
                    for t in range(TT):
                        mm = pe.transpose(job_b[0:3 * GH, P * t:P * t + P],
                                          nparts[:, t, :, :].rearrange("p n h -> p (n h)"), identb[:, :])
                    mm.then_inc(s_np_mm, 1)
                if name == "o":
                    due(pe, s_oT, NG, b, NG)
                    for g in range(NG):
                        mm = pe.transpose(ps_job[:, P * g:P * g + P], oT[:, g, P * k:P * k + P], ident[:, :])
                    mm.then_inc(s_o_mm, 1)
                if name == "yT":
                    due(pe, s_y, TT, b, TT)
                    for t in range(TT):
                        mm = pe.transpose(ps_job[:, P * t:P * t + P], y[:, t, P * k:P * k + P], ident[:, :])
                    mm.then_inc(s_yT_mm, 1)
                if name == "proj":
                    due(pe, s_yT, 2, b, 2)
                    for t in (2 * k, 2 * k + 1):
                        for a in range(CC):
                            mm = pe.matmul(ps_job[:, C * (t % 2):C * (t % 2) + C], yT[:, a, P * t:P * t + P],
                                           wp[:, a, :], start=(a == 0), stop=(a == CC - 1))
                    mm.then_inc(s_pr_mm, 1)
                if name == "x2T":
                    due(pe, s_row, TT, b, TT)
                    for t in range(TT):
                        mm = pe.transpose(ps_job[:, P * t:P * t + P], row[:, t, P * k:P * k + P], ident[:, :])
                    mm.then_inc(s_x2T_mm, 1)
                if name == "lg":
                    due(pe, s_x2T, 2, b, 2)
                    for t in range(TT):
                        for a in range(CC):
                            mm = pe.matmul(ps_job[:, E * t:E * t + E], xn2T[:, a, P * t:P * t + P], wr[:, a, :],
                                           start=(a == 0), stop=(a == CC - 1))
                    mm.then_inc(s_lg_mm, 1)
                if name == "ch":
                    due(pe, s_top, 15, b, 11)
                    for t in range(TT):
                        mm = pe.transpose(job_b[:, P * t:P * t + P],
                                          chosen[:, t, :, :].rearrange("p r e -> p (r e)"), identb[:, :])
                    mm.then_inc(s_ch_mm, 1)

            def body(i, rep):
                on = lambda off: 0 <= rep + off < B
                last = {BANK[j[1], j[2]]: (j, i - 1) for j in jobs(rep - 1)}

                def do(j):
                    _, name, k, off = j
                    bank = BANK[name, k]
                    if bank in last:
                        (_, lname, lk, loff), li = last[bank]
                        taken, per = TAKEN[lname]
                        due(pe, taken, per, li + loff, lk + 1)
                    job(name, k, i + off)
                    last[bank] = (j, i)

                def fill(n, s):
                    par = rep % 2
                    due(pe, s_max, MAXIMA, i, maxima_by(n - 2))
                    for head, qb, at in FILLS[n % len(FILLS)]:
                        h, w = s - s % 2 + head, P * (qb + 1)
                        mm = pe.matmul(ps_max[n % 2][:, at:at + w], Qs[par][0:KROWS, h, P * qb:P * qb + P],
                                       Ks[par][0:KROWS, h, 0:w], start=True, stop=True)
                    mm.then_inc(s_s, 1)

                for s in range(H):
                    todo = jobs(rep, s)
                    fills = list(fills_of(s)) if on(0) else []
                    if on(0) and s % (H // 2) == 0:
                        due(pe, s_stk[s // (H // 2)], 192, i, 192)
                    if fills:
                        fill(fills.pop(0), s)
                    if todo:
                        do(todo.pop(0))
                    if fills:
                        fill(fills.pop(0), s)
                    exp_part(i, rep, on, s)
                    if fills:
                        fill(fills.pop(0), s)
                    value_part(i, rep, on, s)
                    for j in todo:
                        do(j)

            def exp_part(i, rep, on, s):
                if on(-1 if s < LAG else 0):
                    b, h = (i - 1 if s < LAG else i), (s + H - LAG) % H
                    par = (rep - 1 if s < LAG else rep) % 2
                    if h % GH == 0:
                        due(pe, s_nrow[h // GH], 48, b, 48)
                    due(pe, s_exp, H, b, h)
                    for kb in range(TT):
                        at = ST_AT[kb]
                        mm = pe.matmul(ps_exp[:, at:at + T - P * kb], Ks[par][0:MROWS, h, P * kb:P * kb + P],
                                       Qs[par][0:MROWS, h, P * kb:T], start=True, stop=True)
                    mm.then_inc(s_sT, 1)

            def value_part(i, rep, on, s):
                if on(-1 if s < 12 else 0):
                    b = i - 1 if s < 12 else i
                    par = (rep - 1 if s < 12 else rep) % 2
                    g, kb = (s + 4) // GH % NG, s % GH
                    if kb == 0:
                        if g == 0:
                            due(pe, s_v, 2, b, 2)
                        due(pe, s_oT, NG, b, g)
                        due(pe, s_msk, 2 * H, b, 2 * GH * (g + 1))
                    at = ST_AT[kb]
                    for j in range(GH):
                        h = GH * g + j
                        mm = pe.matmul(ps_pv[32 * j:32 * j + 32, P * kb:T], Va[par][:, kb, h, :],
                                       pT[:, h % (2 * GH), at:at + T - P * kb], start=(kb == 0), stop=(kb == TT - 1))
                    if kb == TT - 1:
                        mm.then_inc(s_pv, 1)

            walk(pe, body)

        @block.vector
        def _(dve):
            for k in Ks:
                dve.memset(k[KROWS:P, :, :], 1.0).then_inc(s_ones, 1)

            def norm_stats(src, stats, mv, s_st, s_mv, b):
                for t in range(TT):
                    dve.bn_stats(stats[:, t, :], src[:, t, :]).then_inc(s_st, 1)
                due(dve, s_st, TT, b, TT, apart=s_passed)
                for t in range(TT):
                    dve.bn_aggr(mv[:, t, :], stats[:, t, :]).then_inc(s_mv, 1)

            def norm(out, src, mv, rstd, s_out):
                for t in range(TT):
                    dve.tensor_scalar(out[:, t, 0:C], src[:, t, :], mv[:, t, 0:1], rstd[:, t:t + 1],
                                      ALU.subtract, ALU.mult).then_inc(s_out, 1)

            def stats_1(b):
                due(dve, s_xa, 16, b, 16)
                norm_stats(xa, stats1, mv1, s_st1, s_mv1, b)

            def norm_1(b):
                due(dve, s_rs1, 1, b, 1)
                due(dve, s_xnT_mm, 2, b, 0)
                norm(xn, xa, mv1, rstd1, s_xn)

            dve.wait_ge(s_const, 4)

            def negmax(b, g):
                if g == 0:
                    due(dve, s_np_mm, NG, b, 0)
                else:
                    due(dve, s_np_mm, NG, b, g)
                due(dve, s_max, MAXIMA, b, 4 * GH * (g + 1))
                m = rowmax[:, :, GH * g:GH * g + GH]
                n = 4 * NG
                dve.tensor_scalar(nparts[:, :, 0, :], m, -1.0, None, ALU.mult).then_inc(s_np, 1)
                due(dve, s_np, n, b, 4 * g + 1)
                dve.scalar_tensor_tensor(out=nrest[:, :, :], in0=m, scalar=-1.0, in1=nparts[:, :, 0, :],
                                         op0=ALU.mult, op1=ALU.subtract).then_inc(s_np, 1)
                due(dve, s_np, n, b, 4 * g + 2)
                dve.tensor_copy(nparts[:, :, 1, :], nrest[:, :, :]).then_inc(s_np, 1)
                due(dve, s_np, n, b, 4 * g + 3)
                dve.tensor_tensor(nparts[:, :, 2, :], nrest[:, :, :], nparts[:, :, 1, :],
                                  ALU.subtract).then_inc(s_np, 1)

            def take(name, k, b):
                ps_job = ps_jobs[BANK[name, k]]
                if name == "qk":
                    due(dve, s_p3, 4, b, k - 1)
                    due(dve, s_p1, 4, b, k + 1)
                    dve.tensor_tensor(rest[:, k % 2, :], ps_job[:, :], part[0][:, k, :],
                                      ALU.subtract).then_inc(s_rest, 1)
                if name == "o":
                    due(dve, s_yT_mm, 2, b, 0)
                    due(dve, s_o_mm, TT, b, k + 1)
                    o = ps_job[:, :].rearrange("p (h n) -> p h n", n=2 * D)
                    dve.reciprocal(rsum[:, k, :], o[:, :, D]).then_inc(s_rsum, 1)
                    due(dve, s_rsum, TT, b, k + 1)
                    dve.tensor_tensor(y[:, k, :].rearrange("p (h d) -> p h d", d=D), o[:, :, 0:D],
                                      rsum[:, k, :].unsqueeze(2).to_broadcast([P, H, D]),
                                      ALU.mult).then_inc(s_y, 1)
                if name == "proj":
                    due(dve, s_xb, 16, b, 16)
                    due(dve, s_x2st, 16, b, 0)
                    due(dve, s_pr_mm, 2, b, k + 1)
                    dve.tensor_tensor(x2[:, 2 * k:2 * k + 2, :], ps_job[:, :].rearrange("p (t c) -> p t c", t=2),
                                      xb[:, 2 * k:2 * k + 2, :], ALU.add).then_inc(s_x2, 1)
                if name == "lg":
                    due(dve, s_lg_mm, 1, b, 1)
                    due(dve, s_ex, TT, b, 0)
                    dve.tensor_copy(logit[:, :, :], ps_job[:, 0:TT * E].rearrange("p (t e) -> p t e", e=E))\
                       .then_inc(s_lg, 1)

            def top_choose(b):
                due(dve, s_lg, 1, b, 1, apart=s_passed)
                for t in range(TT):
                    dve.max(top[:, t, :], logit[:, t, :]).then_inc(s_top, 1)
                due(dve, s_top, 15, b, 4, apart=s_passed)
                for t in range(TT):
                    dve.match_replace(cut[:, t, :], top[:, t, :], logit[:, t, :], -3e38).then_inc(s_top, 1)
                dve.tensor_scalar(nmax[:, :], top[:, :, 0], -1.0, None, ALU.mult).then_inc(s_top, 1)
                due(dve, s_ch_mm, 1, b, 0)
                due(dve, s_top, 15, b, 9)
                for r in range(2):
                    dve.tensor_tensor(chosen[:, :, r, :], logit[:, :, :], cut[:, :, :],
                                      ALU.not_equal).then_inc(s_top, 1)

            def top_weights(b):
                due(dve, s_top, 15, b, 11)
                due(dve, s_ex, TT, b, TT)
                dve.tensor_tensor(wts[:, :, :], ex[:, :, :], chosen[:, :, 0, :], ALU.mult).then_inc(s_top, 1)
                due(dve, s_top, 15, b, 12)
                dve.tensor_reduce(wsum[:, :], wts[:, :, :], AX.X, ALU.add).then_inc(s_top, 1)
                due(dve, s_top, 15, b, 13)
                dve.reciprocal(winv[:, :], wsum[:, :]).then_inc(s_top, 1)
                due(dve, s_top, 15, b, 14)
                dve.tensor_tensor(row[:, :, C:ROWW], wts[:, :, :], winv[:, :].unsqueeze(2).to_broadcast([P, TT, E]),
                                  ALU.mult).then_inc(s_top, 1)

            def body(i, rep):
                on = lambda off: 0 <= rep + off < B
                for s in range(H):
                    if s == 0 and on(1):
                        stats_1(i + 1)
                    if on(0):
                        for n in fills_of(s):
                            due(dve, s_s, NF, i, n + 1, apart=s_passed)
                            for head, qb, at in FILLS[n % len(FILLS)]:
                                h, w, o = s - s % 2 + head, P * (qb + 1), T * (n % 2) + at
                                dve.tensor_tensor_reduce(junk[:, o:o + w], ps_max[n % 2][:, at:at + w],
                                                         causal[:, T - w:T], 1.0, 0.0, ALU.add, ALU.max,
                                                         rowmax[:, qb, h:h + 1]).then_inc(s_max, 1)
                    if s % GH == GH - 1 and on(0):
                        negmax(i, s // GH)
                    for _, name, k, off in jobs(rep, s):
                        take(name, k, i + off)
                    if s == 5 and on(-2):
                        due(dve, s_x2, 2, i - 2, 2)
                        norm_stats(x2, stats2, mv2, s_st2, s_mv2, i - 2)
                    if s == 7 and on(-2):
                        due(dve, s_rowst, 16, i - 2, 0)
                        due(dve, s_rs2, 1, i - 2, 1)
                        norm(row, x2, mv2, rstd2, s_row)
                    if s == 10 and on(-2):
                        top_choose(i - 2)
                    if s == 12 and on(-2):
                        top_weights(i - 2)
                    if s == 1 and on(1):
                        norm_1(i + 1)

            walk(dve, body)


def experts(nc, gate, up, down, acc, table_d, maskT_d, out):
    PAIRS = E // 2
    with ExitStack() as ctx:
        def sb(name, shape, dt=F32):
            return ctx.enter_context(nc.sbuf_tensor(name, shape, dt))

        def sem(name):
            return ctx.enter_context(nc.semaphore(name))

        HALF = CAP // 2
        picked = sb("picked", [P, N], BF16)
        count = sb("count", [P, N + CAP])
        ranks = sb("ranks", [P, HALF])
        found = sb("found", [P, HALF], U32)
        spread = sb("spread", [P, CAP])
        pick = sb("pick", [P, E])
        ident = sb("ident2", [P, P])
        src_idx = sb("src_idx", [P, E], I32)
        dst_idx = sb("dst_idx", [P, E], I32)
        gidx = sb("gidx", [P, 4], I32)
        sidx = sb("sidx", [P, 2], I32)
        wg = sb("wg", [P, 2, 2, 2 * I])
        wu = sb("wu", [P, 2, 2, 2 * I])
        wd = sb("wd", [I, 2, 2, C])
        xe = sb("xe", [P, 4, ROWW])
        xeT = sb("xeT", [P, 2, CC, CAP])
        th = sb("th", [I, 2, CAP])
        gated = sb("gated", [I, 2, CAP])
        hT = sb("hT", [I, 2, CAP])
        wcol = sb("wcol", [P, 2])
        ys = sb("ys", [P, 4, C])
        ga = sb("ga", [P, 2, 4, C])
        gb = sb("gb", [P, 2, 4, C])
        res = sb("res", [P, 2, 4, C])

        ps_idx = ctx.enter_context(nc.psum_tensor("ps_idx", [P, 512], F32))
        ps_x = [ctx.enter_context(nc.psum_tensor(f"ps_x{n}", [P, 512], F32)) for n in range(2)]
        ps_h = [ctx.enter_context(nc.psum_tensor(f"ps_h{n}", [P, 512], F32)) for n in range(2)]
        ps_y = [ctx.enter_context(nc.psum_tensor(f"ps_y{n}", [P, 512], F32)) for n in range(2)]

        s_pk = sem("picked_in")
        s_passed = sem("passed2")
        s_cst = sem("consts2_ready")
        s_cf = sem("const2_fill")
        s_cnt = sem("count_ready")
        s_fnd = sem("found_ready")
        s_spr = sem("spread_ready")
        s_idx_mm = sem("idx_in_psum")
        s_idx = sem("idx_ready")
        s_w = [sem(f"expert_weights_in{n}") for n in range(2)]
        s_gi = sem("gather_idx_ready")
        s_si = sem("scatter_idx_ready")
        s_xe = [sem(f"gathered{n}") for n in range(4)]
        s_xT_mm = sem("xeT_in_psum")
        s_xT = sem("xeT_ready")
        s_h_mm = sem("gate_up_in_psum")
        s_th = sem("tanh_ready")
        s_ga = sem("gated_ready")
        s_hT = sem("hT_ready")
        s_y_mm = sem("expert_out_in_psum")
        s_wc = sem("weight_col_ready")
        s_ys = sem("weighted_out_ready")
        s_sc = [sem(f"added{n}") for n in range(2)]
        s_in = [sem(f"sums_in{n}") for n in range(2)]
        s_res = sem("result_ready")
        s_out = [sem(f"result_stored{n}") for n in range(2)]

        block = ctx.enter_context(nc.Block())

        gate_v = gate.rearrange("(q e) (p j) i -> q p e (j i)", e=2, j=CC)
        up_v = up.rearrange("(q e) (p j) i -> q p e (j i)", e=2, j=CC)
        down_v = down.rearrange("(q e) i c -> q i e c", e=2)
        acc_v = [a[0:N, :].rearrange("(b t p) c -> b p t c", t=4, p=P) for a in acc]
        out_v = out.rearrange("b (t p) c -> b p t c", p=P)

        @block.sync
        def _(sp):
            sp.dma_start(picked[:, :].rearrange("p (b t) -> p b t", b=B),
                         maskT_d.rearrange("b p t -> p b t")).then_inc(s_pk, 16)

            def load(q, n):
                sp.dma_start(wg[:, n, :, :], gate_v[q]).then_inc(s_w[n], 16)
                sp.dma_start(wu[:, n, :, :], up_v[q]).then_inc(s_w[n], 16)
                sp.dma_start(wd[:, n, :, :], down_v[q]).then_inc(s_w[n], 16)

            load(0, 0)
            load(1, 1)
            with sp.Fori(1, PAIRS // 2) as r:
                for n in range(2):
                    sp.wait_ge(s_y_mm, r * 4 + (2 * n - 2))
                    load(r * 2 + n, n)
            sp.wait_ge(s_sc[0], 16 * E // 2)
            sp.wait_ge(s_sc[1], 16 * E // 2)
            for b in range(B):
                if b >= 2:
                    sp.wait_ge(s_res, b - 1)
                sp.dma_start(ga[:, b % 2, :, :], acc_v[0][b]).then_inc(s_in[b % 2], 16)
                sp.dma_start(gb[:, b % 2, :, :], acc_v[1][b]).then_inc(s_in[b % 2], 16)
            for n in range(2):
                sp.wait_ge(s_out[n], 16 * B // 2)

        @block.gpsimd
        def _(pool):
            pool.memset(ident[:, :], 0.0).then_inc(s_cf, 1)
            pool.memset(pick[:, :], 0.0).then_inc(s_cf, 1)
            pool.memset(spread[:, :], 0.0).then_inc(s_cf, 1)
            pool.iota(count[:, N:N + CAP], pattern=[[1, CAP]], base=1, channel_multiplier=0,
                      allow_small_or_imprecise_dtypes=True).then_inc(s_cst, 1)
            for n in range(2):
                pool.wait_ge(s_cst, n + 1)
                pool.iota(ranks[HALF * n:HALF * n + HALF, :], pattern=[[1, HALF]], base=1 + HALF * n,
                          channel_multiplier=0, allow_small_or_imprecise_dtypes=True).then_inc(s_cst, 1)
            pool.wait_ge(s_cf, 3)
            pool.wait_ge(s_cst, 3)
            pool.affine_select(out=ident[:, :], in_=ident[:, :], compare_op=ALU.not_equal, fill=1.0, base=0,
                               pattern=[[-1, P]], channel_multiplier=1).then_inc(s_cst, 1)
            for n in range(2):
                pool.wait_ge(s_cst, n + 4)
                half = pick[HALF * n:HALF * n + HALF, :]
                pool.affine_select(out=half, in_=half, compare_op=ALU.not_equal, fill=1.0, base=0,
                                   pattern=[[-1, E]], channel_multiplier=1).then_inc(s_cst, 1)

            def gather(e, k):
                pool.wait_ge(s_gi, e + 1)
                pool.sem_inc(s_passed, 1)
                pool.indirect_dma_start(out=xe[:, k, :], out_offset=None, in_=table_d,
                                        in_offset=bass.IndirectOffsetOnAxis(ap=gidx[:, k:k + 1], axis=0))\
                    .then_inc(s_xe[k], 16)

            def add(e, k):
                n = k % 2
                pool.wait_ge(s_ys, e + 1)
                if not (isinstance(e, int) and e < 2):
                    pool.wait_ge(s_sc[n], add_count(e, k))
                pool.sem_inc(s_passed, 1)
                pool.indirect_dma_start(out=acc[n], out_offset=bass.IndirectOffsetOnAxis(ap=sidx[:, n:n + 1], axis=0),
                                        in_=ys[:, k, :], in_offset=None, bounds_check=N + CAP - 1, oob_is_err=True,
                                        compute_op=ALU.add).then_inc(s_sc[n], 16)

            def add_count(e, k):
                return e * 8 - 8 * (k % 2)

            for k in range(3):
                gather(k, k)
            for k in range(4):
                gather(k + 3, (k + 3) % 4)
                add(k, k)
            with pool.Fori(4, E - 7, 4) as e:
                for k in range(4):
                    gather(e + (k + 3), (k + 3) % 4)
                    add(e + k, k)
            gather(E - 1, 3)
            for k in range(4):
                add(E - 4 + k, k)
            pool.wait_ge(s_sc[0], 16 * E // 2)
            pool.wait_ge(s_sc[1], 16 * E // 2)

        @block.vector
        def _(dve):
            dve.wait_ge(s_pk, 16)
            dve.wait_ge(s_cst, 6)
            dve.tensor_tensor_scan(count[:, 0:N], picked[:, :], picked[:, :], 0.0, ALU.add, ALU.max)\
               .then_inc(s_cnt, 1)
            dve.wait_ge(s_cnt, 1)
            for n in range(HALF // 8):
                dve.max_index(found[:, 8 * n:8 * n + 8], ranks[:, 8 * n:8 * n + 8], count[:, :]).then_inc(s_fnd, 1)
            dve.wait_ge(s_fnd, HALF // 8)
            for n in range(2):
                dve.tensor_copy(spread[HALF * n:HALF * n + HALF, HALF * n:HALF * n + HALF],
                                found[HALF * n:HALF * n + HALF, :]).then_inc(s_spr, 1)
            dve.wait_ge(s_idx_mm, 1)
            dve.tensor_scalar(src_idx[:, :], ps_idx[:, 0:E], float(N - 1), None, ALU.min).then_inc(s_idx, 1)
            dve.tensor_copy(dst_idx[:, :], ps_idx[:, 0:E]).then_inc(s_idx, 1)
            dve.wait_ge(s_idx, 2)

            def index(e, k):
                dve.tensor_copy(gidx[:, k:k + 1], src_idx[:, bass.ds(e, 1)]).then_inc(s_gi, 1)

            for k in range(3):
                index(k, k)

            def hidden(e, n):
                dve.wait_ge(s_th, e + 1)
                dve.scalar_tensor_tensor(out=gated[:, n, :], in0=th[:, n, :], scalar=1.0,
                                         in1=ps_h[n][0:I, 0:CAP], op0=ALU.add, op1=ALU.mult).then_inc(s_ga, 1)
                dve.wait_ge(s_ga, e + 1)
                dve.tensor_tensor(hT[:, n, :], ps_h[n][0:I, CAP:2 * CAP], gated[:, n, :], ALU.mult)\
                   .then_inc(s_hT, 1)

            def weigh(e, k, first):
                n = k % 2
                dve.tensor_copy(wcol[:, n:n + 1], xe[:, k, bass.ds(e + C, 1)]).then_inc(s_wc, 1)
                if not first:
                    dve.wait_ge(s_sc[n], e * 8 - 8 * n)
                dve.tensor_copy(sidx[:, n:n + 1], dst_idx[:, bass.ds(e, 1)]).then_inc(s_si, 1)
                dve.wait_ge(s_wc, e + 1)
                dve.wait_ge(s_y_mm, e + 1)
                dve.tensor_scalar(ys[:, k, :], ps_y[n][:, 0:C], wcol[:, n:n + 1], 0.5, ALU.mult, ALU.mult)\
                   .then_inc(s_ys, 1)

            def step(e, k, first=False, more=True):
                hidden(e, k % 2)
                if more:
                    index(e + 3, (k + 3) % 4)
                weigh(e, k, first)

            for k in range(4):
                step(k, k, first=k < 2)
            with dve.Fori(4, E - 7, 4) as e:
                for k in range(4):
                    step(e + k, k)
            for k in range(4):
                step(E - 4 + k, k, more=k == 0)
            for b in range(B):
                dve.wait_ge(s_in[b % 2], 32 * (b // 2 + 1))
                if b >= 2:
                    dve.wait_ge(s_out[b % 2], 16 * (b // 2))
                dve.tensor_tensor(res[:, b % 2, :, :], ga[:, b % 2, :, :], gb[:, b % 2, :, :], ALU.add)\
                   .then_inc(s_res, 1)

        @block.scalar
        def _(act):
            def step(e, n):
                act.wait_ge(s_xT_mm, e + 1)
                if not (isinstance(e, int) and e < 2):
                    act.wait_ge(s_h_mm, e - 1)
                act.activation(xeT[:, n, :, :].rearrange("p a t -> p (a t)"), ps_x[n][:, 0:2 * CAP],
                               ACT.Copy).then_inc(s_xT, 1)

            def squash(e, n):
                act.wait_ge(s_h_mm, e + 1)
                if not (isinstance(e, int) and e < 2):
                    act.wait_ge(s_ga, e - 1)
                act.activation(th[:, n, :], ps_h[n][0:I, 0:CAP], ACT.Tanh, scale=0.5).then_inc(s_th, 1)

            step(0, 0)
            for e in range(2):
                step(e + 1, (e + 1) % 2)
                squash(e, e)
            with act.Fori(2, E - 2, 2) as e:
                for n in range(2):
                    step(e + (n + 1), (n + 1) % 2)
                    squash(e + n, n)
            step(E - 1, 1)
            squash(E - 2, 0)
            squash(E - 1, 1)
            for b in range(B):
                act.wait_ge(s_res, b + 1)
                act.dma_start(out_v[b], res[:, b % 2, :, :]).then_inc(s_out[b % 2], 16)

        @block.tensor
        def _(pe):
            pe.wait_ge(s_cst, 6)
            pe.wait_ge(s_spr, 2)
            pe.matmul(ps_idx[:, 0:E], spread[:, :], pick[:, :], start=True, stop=True).then_inc(s_idx_mm, 1)

            def turn(e, k, waited, static):
                n = k % 2
                pe.wait_ge(s_xe[k], waited)
                if not static or e >= 2:
                    pe.wait_ge(s_xT, e - 1)
                rows = xe[:, k, 0:C].rearrange("p (m j) -> p j m", j=CC)
                for j in range(CC):
                    mm = pe.transpose(ps_x[n][:, CAP * j:CAP * j + CAP], rows[:, j, :], ident[:, :])
                mm.then_inc(s_xT_mm, 1)

            def gate_up(e, k, wwait, static):
                n = k % 2
                pe.wait_ge(s_w[k // 2], wwait)
                pe.wait_ge(s_xT, e + 1)
                if not static or e >= 2:
                    pe.wait_ge(s_hT, e - 1)
                for m, w in enumerate((wg, wu)):
                    for j in range(CC):
                        mm = pe.matmul(ps_h[n][0:I, CAP * m:CAP * m + CAP], w[:, k // 2, n, I * j:I * j + I],
                                       xeT[:, n, j, :], start=(j == 0), stop=(j == CC - 1))
                mm.then_inc(s_h_mm, 1)

            def project(e, k, static):
                n = k % 2
                pe.wait_ge(s_hT, e + 1)
                if not static or e >= 2:
                    pe.wait_ge(s_ys, e - 1)
                pe.matmul(ps_y[n][:, 0:C], hT[:, n, :], wd[:, k // 2, n, :], start=True, stop=True)\
                  .then_inc(s_y_mm, 1)

            turn(0, 0, 16, True)
            for e in range(4):
                if e < 3:
                    turn(e + 1, e + 1, 16, True)
                else:
                    turn(4, 0, 32, True)
                gate_up(e, e, 48, True)
                if e:
                    project(e - 1, e - 1, True)
            with pe.Fori(1, E // 4 - 1) as r:
                e0 = r * 4
                for k in range(4):
                    turn(e0 + (k + 1), (k + 1) % 4, r * 16 + (16 if k < 3 else 32), False)
                    gate_up(e0 + k, k, r * 48 + 48, False)
                    project(e0 + (k - 1), (k - 1) % 4, False)
            for k in range(4):
                e = E - 4 + k
                if k < 3:
                    turn(e + 1, k + 1, 16 * (E // 4), True)
                gate_up(e, k, 48 * (E // 4), True)
                project(e - 1, (k - 1) % 4, True)
            project(E - 1, 3, True)


def layer_kernel(nc, x, w_attn, w_proj, w_router, gate, up, down, out):
    parts_d = nc.dram_tensor("parts_d", [B, 3, 2 * C, T], BF16, kind="Internal").ap()
    acc = [nc.dram_tensor(f"acc{n}_d", [N + CAP, C], F32, kind="Internal").ap() for n in range(2)]
    table_d = nc.dram_tensor("table_d", [N, ROWW], F32, kind="Internal").ap()
    maskT_d = nc.dram_tensor("maskT_d", [B, P, T], BF16, kind="Internal").ap()
    attention(nc, x, w_attn, w_proj, w_router, parts_d, acc[0], acc[1], table_d, maskT_d)
    experts(nc, gate, up, down, acc, table_d, maskT_d, out)


_INS = ["L0_attn_x", "L0_attn_w_attn", "L0_attn_w_proj", "L0_ffn_router_weight", "L0_ffn_gate_proj",
        "L0_ffn_up_proj", "L0_ffn_down_proj"]
_OUTS = [((B, T, C), "float32")]


def kernel(**inputs):
    import numpy as _np
    import concourse.bacc as _bacc
    from concourse import mybir as _mybir
    from concourse.bass_utils import run_bass_kernel_spmd as _run

    nc = _bacc.Bacc("TRN2", target_bir_lowering=False, num_devices=1)
    arrays, args = {}, []
    for name in _INS:
        a = _np.ascontiguousarray(inputs[name])
        arrays[f"in_{name}_dram"] = a
        args.append(nc.dram_tensor(f"in_{name}_dram", a.shape, _mybir.dt.from_np(a.dtype), kind="ExternalInput").ap())
    for i, (shape, dtype) in enumerate(_OUTS):
        dt = _mybir.dt.from_np(_np.dtype(dtype))
        args.append(nc.dram_tensor(f"out_{i}_dram", shape, dt, kind="ExternalOutput").ap())
    layer_kernel(nc, *args)
    r = _run(nc, [arrays], core_ids=[0])
    got = tuple(r.results[0][f"out_{i}_dram"] for i in range(len(_OUTS)))
    return got[0]
```

```python
from contextlib import ExitStack

import concourse.bass as bass
from concourse import mybir

ALU = mybir.AluOpType
ACT = mybir.ActivationFunctionType
AX = mybir.AxisListType
F32 = mybir.dt.float32
BF16 = mybir.dt.bfloat16
I32 = mybir.dt.int32
U32 = mybir.dt.uint32

P = 128
B = 8
T = 512
C = 256
H = 16
D = 16
E = 64
I = 96
TOPK = 8
CAP = 128
N = B * T
TT = T // P
CC = C // P
GH = 4
NG = H // GH
ROWW = C + E
EPS = 1e-5
SCALE = 0.25
NEG = -1e30
QPART = (0, 0, 0, 1, 1, 2)
KPART = (0, 1, 2, 0, 1, 0)
KROWS = D * len(QPART)
MROWS = KROWS + 3
PAIRS = H // 2
LAG = PAIRS // 2
FILLS = (((0, 3, 0),), ((0, 2, 0), (0, 0, 384)), ((1, 3, 0),), ((1, 2, 0), (1, 0, 384)), ((0, 1, 0), (1, 1, 256)))
FP = len(FILLS)
NF = FP * PAIRS
MAXIMA = 4 * H
MBANKS = 3
ST_AT = {0: 0, 1: 512, 3: 896, 2: 1024}
PW = 1280
KB_OF_PART = ((0, 3), (1, 2))


def due(eng, sem, per, b, k, apart=None):
    if isinstance(b, int):
        if per * b + k > 0:
            eng.wait_ge(sem, per * b + k)
        return
    eng.wait_ge(sem, b * per + k)
    if apart is not None:
        eng.sem_inc(apart, 1)


def before(n):
    return n - MBANKS if n >= MBANKS else max(m for m in range(NF) if m % MBANKS == n) - NF


def maxima_by(n):
    pair, f = divmod(n, len(FILLS))
    return 8 * pair + sum(len(x) for x in FILLS[:f + 1])


def attention(nc, x, w_attn, w_proj, w_router, parts_d, acc0, acc1, table_d, maskT_d):
    x_v = x.rearrange("b (t p) c -> b p t c", p=P)
    acc0_v = acc0[0:N, :].rearrange("(b t p) c -> b p t c", t=TT, p=P)
    table_v = table_d.rearrange("(b t p) c -> b p t c", t=TT, p=P)
    with ExitStack() as ctx:
        def sb(name, shape, dt=F32):
            return ctx.enter_context(nc.sbuf_tensor(name, shape, dt))

        def sem(name):
            return ctx.enter_context(nc.semaphore(name))

        wqkv = sb("wqkv", [P, CC, 3 * C])
        wp = sb("wp", [P, CC, C])
        wr = sb("wr", [P, CC, E])
        ident = sb("ident", [P, P])
        identb = sb("identb", [P, P], BF16)
        causal = sb("causal", [P, T])
        minus_half = sb("minus_half", [P, 2 * TT])
        zeros = sb("zeros", [P, C])
        xa = sb("xa", [P, TT, C])
        xb = sb("xb", [P, TT, C])
        xn = sb("xn", [P, TT, C])
        xnT = sb("xnT", [P, CC, T])
        stats1 = sb("stats1", [P, TT, 6])
        mv1 = sb("mv1", [P, TT, 2])
        ve1 = sb("ve1", [P, TT])
        shift1 = sb("shift1", [P, TT])
        rstd1 = sb("rstd1", [P, TT])
        part = [sb(f"part{n}", [P, 4, T], BF16) for n in range(3)]
        rest = sb("rest", [P, 2, T])
        Qs = [sb(f"Qs{n}", [P, H, T], BF16) for n in range(2)]
        Ks = [sb(f"Ks{n}", [P, H, T], BF16) for n in range(2)]
        Va = [sb(f"Va{n}", [P, TT, H, 2 * D]) for n in range(2)]
        junk = sb("junk", [P, MBANKS * T], BF16)
        rowmax = sb("rowmax", [P, TT, H])
        nrest = sb("nrest", [P, TT, GH])
        nparts = sb("nparts", [P, TT, 3, GH], BF16)
        npT = sb("npT", [3 * GH, T], BF16)
        pT = sb("pT", [P, 2 * GH, PW])
        oT = sb("oT", [P, NG, T])
        rsum = sb("rsum", [P, TT, H])
        y = sb("y", [P, TT, C])
        yT = sb("yT", [P, CC, T])
        x2 = sb("x2", [P, TT, C])
        stats2 = sb("stats2", [P, TT, 6])
        mv2 = sb("mv2", [P, TT, 2])
        ve2 = sb("ve2", [P, TT])
        shift2 = sb("shift2", [P, TT])
        rstd2 = sb("rstd2", [P, TT])
        row = sb("row", [P, TT, ROWW])
        xn2T = sb("xn2T", [P, CC, T])
        logit = sb("logit", [P, TT, E])
        cut = sb("cut", [P, TT, E])
        top = sb("top", [P, TT, TOPK])
        nmax = sb("nmax", [P, TT])
        chosen = sb("chosen", [P, TT, 2, E], BF16)
        ex = sb("ex", [P, TT, E])
        wts = sb("wts", [P, TT, E])
        wsum = sb("wsum", [P, TT])
        winv = sb("winv", [P, TT])
        chosenT = sb("chosenT", [P, T], BF16)

        ps_max = [ctx.enter_context(nc.psum_tensor(f"ps_max{n}", [P, T], F32)) for n in range(MBANKS)]
        ps_exp = [ctx.enter_context(nc.psum_tensor(f"ps_exp{n}", [P, T], F32)) for n in range(2)]
        ps_pv = ctx.enter_context(nc.psum_tensor("ps_pv", [P, T], F32))
        ps_jobs = [ctx.enter_context(nc.psum_tensor(f"ps_job{n}", [P, T], F32)) for n in range(2)]

        s_w = sem("weights_in")
        s_passed = sem("passed")
        s_zero = sem("zeros_ready")
        s_const = sem("consts_ready")
        s_id0 = sem("const_fill")
        s_ones = sem("ones_ready")
        s_vones = sem("v_ones_ready")
        s_acc = sem("accumulators_zeroed")
        s_xa = sem("xa_in")
        s_xb = sem("xb_in")
        s_st1 = sem("stats1_ready")
        s_mv1 = sem("mv1_ready")
        s_ve1 = sem("ve1_ready")
        s_rs1 = sem("rstd1_ready")
        s_sh1 = sem("shift1_ready")
        s_xn = sem("xn_ready")
        s_xnT_mm = sem("xnT_in_psum")
        s_xnT = sem("xnT_ready")
        s_qk_mm = sem("qk_in_psum")
        s_p1 = sem("part1_ready")
        s_rest = sem("rest_ready")
        s_p2 = sem("part2_ready")
        s_p3 = sem("part3_ready")
        s_pst = sem("parts_stored")
        s_stk = [sem(f"stacks_in{n}") for n in range(2)]
        s_v_mm = sem("v_in_psum")
        s_v = sem("v_ready")
        s_s = sem("scores_in_psum")
        s_max = sem("rowmax_ready")
        s_np = sem("negmax_steps")
        s_np_mm = sem("negmaxT_in_psum")
        s_npT = sem("negmaxT_ready")
        s_nrow = [sem(f"negmax_rows_in{g}") for g in range(NG)]
        s_sT = sem("scoresT_in_psum")
        s_exp = sem("exp_ready")
        s_msk = sem("probs_masked")
        s_pv = sem("pv_in_psum")
        s_oT = sem("oT_ready")
        s_o_mm = sem("o_in_psum")
        s_rsum = sem("rowsum_inverse_ready")
        s_y = sem("y_ready")
        s_yT_mm = sem("yT_in_psum")
        s_yT = sem("yT_ready")
        s_pr_mm = sem("proj_in_psum")
        s_x2 = sem("x2_ready")
        s_x2st = sem("x2_stored")
        s_st2 = sem("stats2_ready")
        s_mv2 = sem("mv2_ready")
        s_ve2 = sem("ve2_ready")
        s_rs2 = sem("rstd2_ready")
        s_sh2 = sem("shift2_ready")
        s_row = sem("xn2_ready")
        s_x2T_mm = sem("xn2T_in_psum")
        s_x2T = sem("xn2T_ready")
        s_lg_mm = sem("logits_in_psum")
        s_lg = sem("logits_ready")
        s_top = sem("topk_steps")
        s_ex = sem("router_exp_ready")
        s_rowst = sem("table_stored")
        s_ch_mm = sem("chosenT_in_psum")
        s_ch = sem("chosenT_ready")
        s_chst = sem("chosenT_stored")

        JOBS = [
            (0, 0, "yT", 0, -2), (0, 2, "yT", 1, -2), (0, 4, "npT", 3, -1),
            (1, 0, "proj", 0, -2), (1, 2, "proj", 1, -2), (1, 3, "xnT", 0, 1), (1, 4, "xnT", 1, 1),
            (2, 1, "qk", 0, 1), (2, 2, "npT", 0, 0), (2, 4, "qk", 1, 1),
            (3, 1, "qk", 2, 1), (3, 3, "qk", 3, 1),
            (4, 2, "npT", 1, 0), (4, 3, "x2T", 0, -2), (4, 4, "x2T", 1, -2),
            (5, 1, "lg", 0, -2),
            (6, 0, "v", 0, 1), (6, 2, "npT", 2, 0), (6, 3, "o", 0, -1), (6, 4, "o", 1, -1),
            (7, 0, "v", 1, 1), (7, 1, "o", 2, -1), (7, 2, "o", 3, -1), (7, 3, "ch", 0, -2),
        ]
        ACT_AT = {
            (0, 0): [("oT", 0, -1)], (0, 1): [("yT", 0, -2)], (0, 3): [("yT", 1, -2)],
            (1, 0): [("npT", 3, -1)], (1, 1): [("norm1", 0, 1), ("norm1", 1, 1)],
            (1, 2): [("norm1", 2, 1), ("norm1", 3, 1)], (1, 4): [("xnT", 0, 1)],
            (2, 0): [("xnT", 1, 1), ("oT", 1, -1)], (2, 2): [("part1", 0, 1)], (2, 3): [("npT", 0, 0)],
            (2, 4): [("part2", 0, 1)],
            (3, 0): [("part1", 1, 1)], (3, 1): [("part2", 1, 1)], (3, 2): [("part1", 2, 1)],
            (3, 3): [("part2", 2, 1)], (3, 4): [("part1", 3, 1)],
            (4, 0): [("oT", 2, -1)], (4, 1): [("part2", 3, 1), ("norm2", 0, -2), ("norm2", 1, -2)],
            (4, 2): [("norm2", 2, -2), ("norm2", 3, -2)], (4, 3): [("npT", 1, 0)], (4, 4): [("x2T", 0, -2)],
            (5, 0): [("x2T", 1, -2)], (5, 2): [("lg", 0, -2)],
            (6, 0): [("oT", 3, -1)], (6, 1): [("v", 0, 1)], (6, 3): [("npT", 2, 0)], (6, 4): [("ex", 0, -2)],
            (7, 1): [("v", 1, 1)], (7, 4): [("ch", 0, -2)],
        }
        DVE_AT = {
            (0, 0): [("stat1", 0, 1), ("stat1", 1, 1)], (0, 1): [("stat1", 2, 1), ("stat1", 3, 1)],
            (0, 2): [("aggr1", 0, 1), ("neg0", 3, -1), ("neg1", 3, -1)],
            (0, 3): [("neg2", 3, -1), ("neg3", 3, -1)],
            (1, 0): [("shift1", 0, 1)], (1, 1): [("proj", 0, -2)], (1, 3): [("proj", 1, -2)],
            (2, 0): [("neg0", 0, 0), ("neg1", 0, 0)], (2, 1): [("neg2", 0, 0), ("neg3", 0, 0)],
            (2, 2): [("qk", 0, 1)], (2, 3): [("stat2", 0, -2), ("stat2", 1, -2)],
            (2, 4): [("stat2", 2, -2), ("stat2", 3, -2)],
            (3, 0): [("qk", 1, 1)], (3, 1): [("aggr2", 0, -2)], (3, 2): [("qk", 2, 1)], (3, 3): [("shift2", 0, -2)],
            (4, 0): [("qk", 3, 1), ("neg0", 1, 0)], (4, 1): [("neg1", 1, 0), ("neg2", 1, 0), ("neg3", 1, 0)],
            (5, 3): [("top8", 0, -2)], (5, 4): [("cut", 0, -2)],
            (6, 0): [("neg0", 2, 0), ("neg1", 2, 0)], (6, 1): [("neg2", 2, 0), ("neg3", 2, 0)],
            (6, 2): [("choose", 0, -2)], (6, 4): [("o", 0, -1)],
            (7, 0): [("o", 1, -1)], (7, 1): [("w0", 0, -2), ("w1", 0, -2)], (7, 2): [("o", 2, -1), ("w2", 0, -2)],
            (7, 3): [("o", 3, -1), ("w3", 0, -2)],
        }
        POOL_AT = {
            (0, 3): [("rstd1", 0, 1)], (3, 0): [("part3", 0, 1)], (3, 2): [("rstd2", 0, -2), ("part3", 1, 1)],
            (4, 0): [("part3", 2, 1)], (4, 2): [("part3", 3, 1)],
        }
        TAKEN = {"xnT": (s_xnT, 2), "qk": (s_rest, 4), "v": (s_v, 2), "npT": (s_npT, 4), "o": (s_y, 4),
                 "yT": (s_yT, 2), "proj": (s_x2, 2), "x2T": (s_x2T, 2), "lg": (s_lg, 1), "ch": (s_ch, 1)}

        BANK = {(name, k): n % 2 for n, (_, _, name, k, _) in enumerate(JOBS)}

        def there(rep, off):
            return 0 <= rep + off < B

        def expo(i, rep, p):
            if p < LAG:
                return (i - 1, (rep - 1) % 2, 2 * (p + LAG)) if there(rep, -1) else None
            return (i, rep % 2, 2 * (p - LAG)) if there(rep, 0) else None

        def walk(eng, body):
            for i in range(-1, 3):
                body(i, i)
            with eng.Fori(3, B - 2, 2) as i:
                body(i, 3)
                body(i + 1, 4)
            for i in range(B - 1, B + 2):
                body(i, i)

        block = ctx.enter_context(nc.Block())

        @block.sync
        def _(sp):
            def body(i, rep):
                on = lambda off: 0 <= rep + off < B

                def negmax_rows(b, par, g):
                    due(sp, s_npT, NG, b, g + 1)
                    for n in range(3):
                        sp.dma_start(Qs[par][KROWS + n:KROWS + n + 1, GH * g:GH * g + GH, :],
                                     npT[GH * n:GH * n + GH, :]).then_inc(s_nrow[g], 16)

                if on(1):
                    due(sp, s_xn, TT, i, TT)
                    sp.dma_start(xa[:, :, :], x_v[i + 1]).then_inc(s_xa, 16)
                if on(-1):
                    negmax_rows(i - 1, (rep - 1) % 2, 3)
                if on(-2):
                    due(sp, s_x2, 2, i - 3, 2)
                    sp.dma_start(xb[:, :, :], x_v[i - 2]).then_inc(s_xb, 16)
                if on(-2):
                    due(sp, s_x2, 2, i - 2, 2)
                    sp.dma_start(acc0_v[i - 2], x2[:, :, :]).then_inc(s_x2st, 16)
                if on(0):
                    negmax_rows(i, rep % 2, 0)
                if on(1):
                    due(sp, s_p3, 4, i + 1, 4)
                    for n in range(3):
                        sp.dma_start(parts_d[i + 1, n].rearrange("(g p) t -> p g t", p=P),
                                     part[n][:, :, :]).then_inc(s_pst, 16)
                if on(0):
                    negmax_rows(i, rep % 2, 1)
                if on(1):
                    due(sp, s_pst, 48, i + 1, 48, apart=s_passed)
                    par = (rep + 1) % 2
                    for half in range(2):
                        if on(-1) and half == 0:
                            due(sp, s_sT, NF, i - 1, NF)
                        if on(0) and half == 1:
                            due(sp, s_s, NF, i, NF // 2 + 1)
                        h0 = half * H // 2
                        for st, off, which in ((Ks, C, KPART), (Qs, 0, QPART)):
                            for n, m in enumerate(which):
                                src = parts_d[i + 1, m, off:off + C, :].rearrange("(h d) t -> d h t", d=D)
                                sp.dma_start(st[par][D * n:D * n + D, h0:h0 + H // 2, :],
                                             src[:, h0:h0 + H // 2, :]).then_inc(s_stk[half], 16)
                if on(0):
                    negmax_rows(i, rep % 2, 2)
                if isinstance(i, int) and i == 0:
                    sp.wait_ge(s_zero, 1)
                    sp.dma_start(acc0[N:N + P, :], zeros[:, :]).then_inc(s_acc, 16)
                    sp.dma_start(acc1.rearrange("(t p) c -> p t c", p=P),
                                 zeros[:, :].unsqueeze(1).to_broadcast([P, N // P + 1, C])).then_inc(s_acc, 16)
                if on(-2):
                    due(sp, s_top, 15, i - 2, 15)
                    sp.dma_start(table_v[i - 2], row[:, :, :]).then_inc(s_rowst, 16)
                    due(sp, s_ch, 1, i - 2, 1)
                    sp.dma_start(maskT_d[i - 2], chosenT[:, :]).then_inc(s_chst, 16)

            walk(sp, body)
            sp.wait_ge(s_acc, 32)
            sp.wait_ge(s_x2st, 16 * B)
            sp.wait_ge(s_rowst, 16 * B)
            sp.wait_ge(s_chst, 16 * B)

        @block.gpsimd
        def _(pool):
            pool.memset(zeros[:, :], 0.0).then_inc(s_zero, 1)
            for m in (ident, identb, causal):
                pool.memset(m[:, :], 0.0).then_inc(s_id0, 1)
            pool.memset(minus_half[:, :], -0.5).then_inc(s_const, 1)
            pool.wait_ge(s_id0, 3)
            for m in (ident, identb):
                pool.affine_select(out=m[:, :], in_=m[:, :], compare_op=ALU.not_equal, fill=1.0, base=0,
                                   pattern=[[-1, P]], channel_multiplier=1).then_inc(s_const, 1)
            diag = causal[:, T - P:T]
            pool.affine_select(out=diag, in_=diag, compare_op=ALU.is_ge, fill=NEG, base=0,
                               pattern=[[-1, P]], channel_multiplier=1).then_inc(s_const, 1)
            for v in Va:
                pool.memset(v[:, :, :, D:2 * D], 1.0).then_inc(s_vones, 1)
            pool.wait_ge(s_const, 4)

            def rstd(s_mv, s_ve, s_rs, mv, ve, out, b):
                due(pool, s_mv, TT, b, TT, apart=s_passed)
                pool.tensor_scalar(ve[:, :], mv[:, :, 1], EPS, None, ALU.add).then_inc(s_ve, 1)
                due(pool, s_ve, 1, b, 1)
                pool.tensor_tensor(out[:, :], ve[:, :], minus_half[:, 0:TT], ALU.pow).then_inc(s_rs, 1)

            def body(i, rep):
                for p in range(PAIRS):
                    for f in range(FP):
                        if (e := expo(i, rep, p)) is not None:
                            b, _, h0 = e
                            n = FP * (h0 // 2) + f
                            if f == FP - 1:
                                at = h0 % (2 * GH)
                                diag, blocks = pT[:, at:at + 2, ST_AT[2]:ST_AT[2] + P], 2
                            else:
                                v = pT[:, (h0 + f // 2) % (2 * GH), :].rearrange("p (a n) -> p a n", n=P)
                                diag, blocks = (v[:, 0:1, :], 1) if f % 2 == 0 else (v[:, 4:8:3, :], 2)
                            due(pool, s_exp, NF, b, n + 1, apart=s_passed)
                            pool.affine_select(out=diag, in_=diag, compare_op=ALU.is_ge, fill=0.0, base=0,
                                               pattern=[[0, blocks], [1, P]], channel_multiplier=-1)\
                                .then_inc(s_msk, 1)
                        for name, k, off in POOL_AT.get((p, f), ()):
                            if not there(rep, off):
                                continue
                            b = i + off
                            if name == "rstd1":
                                due(pool, s_xn, TT, b, 0)
                                rstd(s_mv1, s_ve1, s_rs1, mv1, ve1, rstd1, b)
                            if name == "rstd2":
                                due(pool, s_row, TT, b, 0)
                                rstd(s_mv2, s_ve2, s_rs2, mv2, ve2, rstd2, b)
                            if name == "part3":
                                due(pool, s_pst, 48, b, 0)
                                due(pool, s_p2, 4, b, k + 1)
                                pool.tensor_tensor(part[2][:, k, :], rest[:, k % 2, :], part[1][:, k, :],
                                                   ALU.subtract).then_inc(s_p3, 1)

            walk(pool, body)

        @block.scalar
        def _(act):
            act.dma_start(wqkv[:, :, :], w_attn.rearrange("(a p) n -> p a n", p=P)).then_inc(s_w, 16)
            act.dma_start(wp[:, :, :], w_proj.rearrange("(a p) n -> p a n", p=P)).then_inc(s_w, 16)
            act.dma_start(wr[:, :, :], w_router.rearrange("(a p) n -> p a n", p=P)).then_inc(s_w, 16)
            act.wait_ge(s_vones, 2)

            def norm(out, src, shift, rstd, s_in, s_out, b, t):
                due(act, s_in, 1, b, 1)
                act.activation(out[:, t, 0:C], src[:, t, :], ACT.Identity, bias=shift[:, t:t + 1],
                               scale=rstd[:, t:t + 1]).then_inc(s_out, 1)

            def take(name, k, b, par):
                ps_job = ps_jobs[BANK.get(("qk" if name == "part1" else name, k), 0)]
                job_b = ps_job[:, :].bitcast(BF16)
                if name == "norm1":
                    due(act, s_xnT_mm, 2, b, 0)
                    norm(xn, xa, shift1, rstd1, s_sh1, s_xn, b, k)
                if name == "norm2":
                    due(act, s_rowst, 16, b, 0)
                    norm(row, x2, shift2, rstd2, s_sh2, s_row, b, k)
                if name == "oT":
                    due(act, s_o_mm, TT, b, 0)
                    due(act, s_pv, NG, b, k + 1)
                    act.activation(oT[:, k, :], ps_pv[:, :], ACT.Copy).then_inc(s_oT, 1)
                if name == "ex":
                    due(act, s_top, 15, b, 9)
                    for t in range(TT):
                        act.activation(ex[:, t, :], logit[:, t, :], ACT.Exp, bias=nmax[:, t:t + 1])\
                           .then_inc(s_ex, 1)
                if name == "lg":
                    due(act, s_top, 15, b, 0)
                    due(act, s_lg_mm, 1, b, 1)
                    act.activation(logit[:, :, :], ps_job[:, 0:TT * E].rearrange("p (t e) -> p t e", e=E),
                                   ACT.Copy).then_inc(s_lg, 1)
                if name == "xnT":
                    due(act, s_v_mm, 2, b, 0)
                    due(act, s_xnT_mm, 2, b, k + 1)
                    act.activation(xnT[:, k, :], ps_job[:, :], ACT.Copy).then_inc(s_xnT, 1)
                if name == "part1":
                    due(act, s_pst, 48, b, 0)
                    due(act, s_qk_mm, 4, b, k + 1)
                    act.activation(part[0][:, k, :], ps_job[:, :], ACT.Copy).then_inc(s_p1, 1)
                if name == "part2":
                    due(act, s_rest, 4, b, k + 1)
                    act.activation(part[1][:, k, :], rest[:, k % 2, :], ACT.Copy).then_inc(s_p2, 1)
                if name == "v":
                    due(act, s_pv, NG, b - 2, NG)
                    due(act, s_v_mm, 2, b, k + 1)
                    act.activation(Va[par][:, 2 * k:2 * k + 2, :, 0:D],
                                   ps_job[:, :].rearrange("p (t h d) -> p t h d", t=2, d=D),
                                   ACT.Copy).then_inc(s_v, 1)
                if name == "npT":
                    if k == 0:
                        due(act, s_nrow[NG - 1], 48, b, 0)
                    else:
                        due(act, s_nrow[k - 1], 48, b, 48)
                    due(act, s_np_mm, NG, b, k + 1)
                    act.activation(npT[:, :], job_b[0:3 * GH, 0:T], ACT.Copy).then_inc(s_npT, 1)
                if name == "yT":
                    due(act, s_pr_mm, 2, b, 0)
                    due(act, s_yT_mm, 2, b, k + 1)
                    act.activation(yT[:, k, :], ps_job[:, :], ACT.Copy).then_inc(s_yT, 1)
                if name == "x2T":
                    due(act, s_lg_mm, 1, b, 0)
                    due(act, s_x2T_mm, 2, b, k + 1)
                    act.activation(xn2T[:, k, :], ps_job[:, :], ACT.Copy).then_inc(s_x2T, 1)
                if name == "ch":
                    due(act, s_chst, 16, b, 0)
                    due(act, s_ch_mm, 1, b, 1)
                    act.activation(chosenT[:, :], job_b[:, 0:T], ACT.Copy).then_inc(s_ch, 1)

            def body(i, rep):
                for p in range(PAIRS):
                    for f in range(FP):
                        if (e := expo(i, rep, p)) is not None:
                            b, _, h0 = e
                            n = FP * (h0 // 2) + f
                            if f == 0:
                                due(act, s_pv, NG, b, h0 // GH - 1)
                            due(act, s_sT, NF, b, n + 1)
                            at = (h0 + f // 2) % (2 * GH)
                            if f == FP - 1:
                                at = h0 % (2 * GH)
                                dst = pT[:, at:at + 2, ST_AT[2]:PW]
                                src = ps_exp[n % 2][:, :].rearrange("p (h n) -> p h n", h=2)
                            else:
                                c = T * (f % 2)
                                dst, src = pT[:, at, c:c + T], ps_exp[n % 2][:, :]
                            act.activation(dst, src, ACT.Exp, scale=SCALE).then_inc(s_exp, 1)
                        for name, k, off in ACT_AT.get((p, f), ()):
                            if there(rep, off):
                                take(name, k, i + off, (rep + off) % 2)

            walk(act, body)

        @block.tensor
        def _(pe):
            pe.wait_ge(s_const, 4)
            pe.wait_ge(s_w, 48)
            pe.wait_ge(s_ones, 2)
            pe.wait_ge(s_vones, 2)

            def job(name, k, b):
                ps_job = ps_jobs[BANK[name, k]]
                job_b = ps_job[:, :].bitcast(BF16)
                if name == "xnT":
                    due(pe, s_xn, TT, b, TT)
                    for t in range(TT):
                        mm = pe.transpose(ps_job[:, P * t:P * t + P], xn[:, t, P * k:P * k + P], ident[:, :])
                    mm.then_inc(s_xnT_mm, 1)
                if name == "qk":
                    due(pe, s_xnT, 2, b, 2)
                    for a in range(CC):
                        mm = pe.matmul(ps_job[:, :], wqkv[:, a, P * k:P * k + P], xnT[:, a, :],
                                       start=(a == 0), stop=(a == CC - 1))
                    mm.then_inc(s_qk_mm, 1)
                if name == "v":
                    for t in (2 * k, 2 * k + 1):
                        for a in range(CC):
                            mm = pe.matmul(ps_job[:, C * (t % 2):C * (t % 2) + C], xnT[:, a, P * t:P * t + P],
                                           wqkv[:, a, 2 * C:3 * C], start=(a == 0), stop=(a == CC - 1))
                    mm.then_inc(s_v_mm, 1)
                if name == "npT":
                    due(pe, s_np, 4 * NG, b, 4 * k + 4)
                    for t in range(TT):
                        mm = pe.transpose(job_b[0:3 * GH, P * t:P * t + P],
                                          nparts[:, t, :, :].rearrange("p n h -> p (n h)"), identb[:, :])
                    mm.then_inc(s_np_mm, 1)
                if name == "o":
                    due(pe, s_oT, NG, b, NG)
                    for g in range(NG):
                        mm = pe.transpose(ps_job[:, P * g:P * g + P], oT[:, g, P * k:P * k + P], ident[:, :])
                    mm.then_inc(s_o_mm, 1)
                if name == "yT":
                    due(pe, s_y, TT, b, TT)
                    for t in range(TT):
                        mm = pe.transpose(ps_job[:, P * t:P * t + P], y[:, t, P * k:P * k + P], ident[:, :])
                    mm.then_inc(s_yT_mm, 1)
                if name == "proj":
                    due(pe, s_yT, 2, b, 2)
                    for t in (2 * k, 2 * k + 1):
                        for a in range(CC):
                            mm = pe.matmul(ps_job[:, C * (t % 2):C * (t % 2) + C], yT[:, a, P * t:P * t + P],
                                           wp[:, a, :], start=(a == 0), stop=(a == CC - 1))
                    mm.then_inc(s_pr_mm, 1)
                if name == "x2T":
                    due(pe, s_row, TT, b, TT)
                    for t in range(TT):
                        mm = pe.transpose(ps_job[:, P * t:P * t + P], row[:, t, P * k:P * k + P], ident[:, :])
                    mm.then_inc(s_x2T_mm, 1)
                if name == "lg":
                    due(pe, s_x2T, 2, b, 2)
                    for t in range(TT):
                        for a in range(CC):
                            mm = pe.matmul(ps_job[:, E * t:E * t + E], xn2T[:, a, P * t:P * t + P], wr[:, a, :],
                                           start=(a == 0), stop=(a == CC - 1))
                    mm.then_inc(s_lg_mm, 1)
                if name == "ch":
                    due(pe, s_top, 15, b, 11)
                    for t in range(TT):
                        mm = pe.transpose(job_b[:, P * t:P * t + P],
                                          chosen[:, t, :, :].rearrange("p r e -> p (r e)"), identb[:, :])
                    mm.then_inc(s_ch_mm, 1)

            def body(i, rep):
                last = {BANK[j[2], j[3]]: (j, i - 1) for j in JOBS if there(rep - 1, j[4])}
                for p in range(PAIRS):
                    for f in range(FP):
                        if there(rep, 0):
                            if f == 0 and p % (PAIRS // 2) == 0:
                                due(pe, s_stk[p // (PAIRS // 2)], 192, i, 192)
                            max_fill(i, rep % 2, p, f)
                        if (e := expo(i, rep, p)) is not None:
                            exp_fill(*e, f)
                        for j in JOBS:
                            _, _, name, k, off = j
                            if j[0:2] != (p, f) or not there(rep, off):
                                continue
                            bank = BANK[name, k]
                            if bank in last:
                                (_, _, lname, lk, loff), li = last[bank]
                                taken, per = TAKEN[lname]
                                due(pe, taken, per, li + loff, lk + 1)
                            job(name, k, i + off)
                            last[bank] = (j, i)
                        if f in (1, 3):
                            off = 0 if p >= 6 else -1
                            if there(rep, off):
                                g = (p + 2) // 2 % NG
                                value_part(i + off, (rep + off) % 2, g, p % 2, f // 2)

            def max_fill(b, par, p, f):
                n = FP * p + f
                due(pe, s_max, MAXIMA, b, maxima_by(before(n)))
                for head, qb, at in FILLS[f]:
                    h, w = 2 * p + head, P * (qb + 1)
                    mm = pe.matmul(ps_max[n % MBANKS][:, at:at + w], Qs[par][0:KROWS, h, P * qb:P * qb + P],
                                   Ks[par][0:KROWS, h, 0:w], start=True, stop=True)
                mm.then_inc(s_s, 1)

            def exp_fill(b, par, h0, f):
                n = FP * (h0 // 2) + f
                if f == 0 and h0 % GH == 0:
                    due(pe, s_nrow[h0 // GH], 48, b, 48)
                due(pe, s_exp, NF, b, n - 1)
                for head, block, at in FILLS[f]:
                    h, kb = h0 + head, 3 - block
                    w = T - P * kb
                    mm = pe.matmul(ps_exp[n % 2][:, at:at + w], Ks[par][0:MROWS, h, P * kb:P * kb + P],
                                   Qs[par][0:MROWS, h, P * kb:T], start=True, stop=True)
                mm.then_inc(s_sT, 1)

            def value_part(b, par, g, step, half):
                kb = KB_OF_PART[step][half]
                if kb == 0:
                    if g == 0:
                        due(pe, s_v, 2, b, 2)
                    due(pe, s_oT, NG, b, g)
                    due(pe, s_msk, NF, b, 2 * FP * (g + 1))
                at = ST_AT[kb]
                for j in range(GH):
                    h = GH * g + j
                    mm = pe.matmul(ps_pv[32 * j:32 * j + 32, P * kb:T], Va[par][:, kb, h, :],
                                   pT[:, h % (2 * GH), at:at + T - P * kb], start=(kb == 0),
                                   stop=(step == 1 and half == 1))
                if step == 1 and half == 1:
                    mm.then_inc(s_pv, 1)

            walk(pe, body)

        @block.vector
        def _(dve):
            for k in Ks:
                dve.memset(k[KROWS:P, :, :], 1.0).then_inc(s_ones, 1)

            dve.wait_ge(s_const, 4)

            def negmax(b, g, step):
                m = rowmax[:, :, GH * g:GH * g + GH]
                if step == 0:
                    due(dve, s_np_mm, NG, b, g)
                    due(dve, s_max, MAXIMA, b, 4 * GH * (g + 1))
                    dve.tensor_scalar(nparts[:, :, 0, :], m, -1.0, None, ALU.mult).then_inc(s_np, 1)
                    return
                due(dve, s_np, 4 * NG, b, 4 * g + step)
                if step == 1:
                    dve.scalar_tensor_tensor(out=nrest[:, :, :], in0=m, scalar=-1.0, in1=nparts[:, :, 0, :],
                                             op0=ALU.mult, op1=ALU.subtract).then_inc(s_np, 1)
                if step == 2:
                    dve.tensor_copy(nparts[:, :, 1, :], nrest[:, :, :]).then_inc(s_np, 1)
                if step == 3:
                    dve.tensor_tensor(nparts[:, :, 2, :], nrest[:, :, :], nparts[:, :, 1, :],
                                      ALU.subtract).then_inc(s_np, 1)

            def norm_step(name, k, b):
                one = name[-1] == "1"
                src, stats, mv, rstd, shift = (xa, stats1, mv1, rstd1, shift1) if one else \
                    (x2, stats2, mv2, rstd2, shift2)
                s_st, s_mv, s_rs, s_sh = (s_st1, s_mv1, s_rs1, s_sh1) if one else (s_st2, s_mv2, s_rs2, s_sh2)
                if name[:-1] == "stat":
                    if one:
                        due(dve, s_xa, 16, b, 16)
                    else:
                        due(dve, s_x2, 2, b, 2)
                    dve.bn_stats(stats[:, k, :], src[:, k, :]).then_inc(s_st, 1)
                if name[:-1] == "aggr":
                    due(dve, s_st, TT, b, TT, apart=s_passed)
                    for t in range(TT):
                        dve.bn_aggr(mv[:, t, :], stats[:, t, :]).then_inc(s_mv, 1)
                if name[:-1] == "shift":
                    due(dve, s_rs, 1, b, 1)
                    dve.scalar_tensor_tensor(out=shift[:, :], in0=mv[:, :, 0], scalar=-1.0, in1=rstd[:, :],
                                             op0=ALU.mult, op1=ALU.mult).then_inc(s_sh, 1)

            def take(name, k, b):
                ps_job = ps_jobs[BANK.get((name, k), 0)]
                if name == "qk":
                    due(dve, s_p3, 4, b, k - 1)
                    due(dve, s_p1, 4, b, k + 1)
                    dve.tensor_tensor(rest[:, k % 2, :], ps_job[:, :], part[0][:, k, :],
                                      ALU.subtract).then_inc(s_rest, 1)
                if name == "o":
                    due(dve, s_yT_mm, 2, b, 0)
                    due(dve, s_o_mm, TT, b, k + 1)
                    o = ps_job[:, :].rearrange("p (h n) -> p h n", n=2 * D)
                    dve.reciprocal(rsum[:, k, :], o[:, :, D]).then_inc(s_rsum, 1)
                    due(dve, s_rsum, TT, b, k + 1)
                    dve.tensor_tensor(y[:, k, :].rearrange("p (h d) -> p h d", d=D), o[:, :, 0:D],
                                      rsum[:, k, :].unsqueeze(2).to_broadcast([P, H, D]),
                                      ALU.mult).then_inc(s_y, 1)
                if name == "proj":
                    due(dve, s_xb, 16, b, 16)
                    due(dve, s_x2st, 16, b, 0)
                    due(dve, s_row, TT, b, 0)
                    due(dve, s_pr_mm, 2, b, k + 1)
                    dve.tensor_tensor(x2[:, 2 * k:2 * k + 2, :], ps_job[:, :].rearrange("p (t c) -> p t c", t=2),
                                      xb[:, 2 * k:2 * k + 2, :], ALU.add).then_inc(s_x2, 1)
                if name == "top8":
                    due(dve, s_lg, 1, b, 1, apart=s_passed)
                    for t in range(TT):
                        dve.max(top[:, t, :], logit[:, t, :]).then_inc(s_top, 1)
                if name == "cut":
                    due(dve, s_top, 15, b, 4, apart=s_passed)
                    for t in range(TT):
                        dve.match_replace(cut[:, t, :], top[:, t, :], logit[:, t, :], -3e38).then_inc(s_top, 1)
                    due(dve, s_ex, TT, b, 0)
                    dve.tensor_scalar(nmax[:, :], top[:, :, 0], -1.0, None, ALU.mult).then_inc(s_top, 1)
                if name == "choose":
                    due(dve, s_ch_mm, 1, b, 0)
                    due(dve, s_top, 15, b, 9)
                    for r in range(2):
                        dve.tensor_tensor(chosen[:, :, r, :], logit[:, :, :], cut[:, :, :],
                                          ALU.not_equal).then_inc(s_top, 1)
                if name == "w0":
                    due(dve, s_top, 15, b, 11)
                    due(dve, s_ex, TT, b, TT)
                    dve.tensor_tensor(wts[:, :, :], ex[:, :, :], chosen[:, :, 0, :], ALU.mult).then_inc(s_top, 1)
                if name == "w1":
                    due(dve, s_top, 15, b, 12)
                    dve.tensor_reduce(wsum[:, :], wts[:, :, :], AX.X, ALU.add).then_inc(s_top, 1)
                if name == "w2":
                    due(dve, s_top, 15, b, 13)
                    dve.reciprocal(winv[:, :], wsum[:, :]).then_inc(s_top, 1)
                if name == "w3":
                    due(dve, s_rowst, 16, b, 0)
                    due(dve, s_top, 15, b, 14)
                    dve.tensor_tensor(row[:, :, C:ROWW], wts[:, :, :],
                                      winv[:, :].unsqueeze(2).to_broadcast([P, TT, E]), ALU.mult).then_inc(s_top, 1)

            def body(i, rep):
                for p in range(PAIRS):
                    for f in range(FP):
                        if there(rep, 0):
                            n = FP * p + f
                            due(dve, s_s, NF, i, n + 1, apart=s_passed)
                            for head, qb, at in FILLS[f]:
                                h, w, o = 2 * p + head, P * (qb + 1), T * (n % MBANKS) + at
                                dve.tensor_tensor_reduce(junk[:, o:o + w], ps_max[n % MBANKS][:, at:at + w],
                                                         causal[:, T - w:T], 1.0, 0.0, ALU.add, ALU.max,
                                                         rowmax[:, qb, h:h + 1]).then_inc(s_max, 1)
                        for name, k, off in DVE_AT.get((p, f), ()):
                            if not there(rep, off):
                                continue
                            if name[:3] == "neg":
                                negmax(i + off, k, int(name[3]))
                            elif name[:-1] in ("stat", "aggr", "shift"):
                                norm_step(name, k, i + off)
                            else:
                                take(name, k, i + off)

            walk(dve, body)


def experts(nc, gate, up, down, acc, table_d, maskT_d, out):
    GRP = 4
    RING = 2 * GRP
    LEAD = 6
    with ExitStack() as ctx:
        def sb(name, shape, dt=F32):
            return ctx.enter_context(nc.sbuf_tensor(name, shape, dt))

        def sem(name):
            return ctx.enter_context(nc.semaphore(name))

        HALF = CAP // 2
        picked = sb("picked", [P, N], BF16)
        count = sb("count", [P, N + CAP])
        ranks = sb("ranks", [P, HALF])
        found = sb("found", [P, HALF], U32)
        spread = sb("spread", [P, CAP])
        pick = sb("pick", [P, E])
        ident = sb("ident2", [P, P])
        src_idx = sb("src_idx", [P, E], I32)
        dst_idx = sb("dst_idx", [P, E], I32)
        gidx = sb("gidx", [P, RING], I32)
        sidx = sb("sidx", [P, RING], I32)
        wg = sb("wg", [P, 2, GRP, 2 * I])
        wu = sb("wu", [P, 2, GRP, 2 * I])
        wd = sb("wd", [I, 2, GRP, C])
        xe = sb("xe", [P, RING, ROWW])
        xeT = sb("xeT", [P, 2, CC, CAP])
        th = sb("th", [I, 2, CAP])
        gated = sb("gated", [I, 2, CAP])
        hT = sb("hT", [I, 2, CAP])
        wcol = sb("wcol", [P, 2])
        ys = sb("ys", [P, 4, C])
        ga = sb("ga", [P, 2, 4, C])
        gb = sb("gb", [P, 2, 4, C])
        res = sb("res", [P, 2, 4, C])

        ps_idx = ctx.enter_context(nc.psum_tensor("ps_idx", [P, 512], F32))
        ps_x = [ctx.enter_context(nc.psum_tensor(f"ps_x{n}", [P, 512], F32)) for n in range(2)]
        ps_h = [ctx.enter_context(nc.psum_tensor(f"ps_h{n}", [P, 512], F32)) for n in range(2)]
        ps_y = [ctx.enter_context(nc.psum_tensor(f"ps_y{n}", [P, 512], F32)) for n in range(2)]

        s_pk = sem("picked_in")
        s_passed = sem("passed2")
        s_cst = sem("consts2_ready")
        s_cf = sem("const2_fill")
        s_cnt = sem("count_ready")
        s_fnd = sem("found_ready")
        s_spr = sem("spread_ready")
        s_idx_mm = sem("idx_in_psum")
        s_idx = sem("idx_ready")
        s_w = [sem(f"expert_weights_in{n}") for n in range(2)]
        s_gi = sem("gather_idx_ready")
        s_si = sem("scatter_idx_ready")
        s_xe = [sem(f"gathered{n}") for n in range(RING)]
        s_xT_mm = sem("xeT_in_psum")
        s_xT = sem("xeT_ready")
        s_h_mm = sem("gate_up_in_psum")
        s_th = sem("tanh_ready")
        s_ga = sem("gated_ready")
        s_hT = sem("hT_ready")
        s_y_mm = sem("expert_out_in_psum")
        s_wc = sem("weight_col_ready")
        s_ys = sem("weighted_out_ready")
        s_sc = [sem(f"added{n}") for n in range(2)]
        s_in = [sem(f"sums_in{n}") for n in range(2)]
        s_res = sem("result_ready")
        s_out = [sem(f"result_stored{n}") for n in range(2)]

        block = ctx.enter_context(nc.Block())

        gate_v = gate.rearrange("(q e) (p j) i -> q p e (j i)", e=GRP, j=CC)
        up_v = up.rearrange("(q e) (p j) i -> q p e (j i)", e=GRP, j=CC)
        down_v = down.rearrange("(q e) i c -> q i e c", e=GRP)
        acc_v = [a[0:N, :].rearrange("(b t p) c -> b p t c", t=4, p=P) for a in acc]
        out_v = out.rearrange("b (t p) c -> b p t c", p=P)

        @block.sync
        def _(sp):
            sp.dma_start(picked[:, :].rearrange("p (b t) -> p b t", b=B),
                         maskT_d.rearrange("b p t -> p b t")).then_inc(s_pk, 16)

            def load(q, n):
                sp.dma_start(wg[:, n, :, :], gate_v[q]).then_inc(s_w[n], 16)
                sp.dma_start(wu[:, n, :, :], up_v[q]).then_inc(s_w[n], 16)
                sp.dma_start(wd[:, n, :, :], down_v[q]).then_inc(s_w[n], 16)

            load(0, 0)
            load(1, 1)
            with sp.Fori(1, E // RING) as r:
                for n in range(2):
                    sp.wait_ge(s_y_mm, r * RING + (GRP * (n + 1) - RING))
                    load(r * 2 + n, n)
            sp.wait_ge(s_sc[0], 16 * E // 2)
            sp.wait_ge(s_sc[1], 16 * E // 2)
            for b in range(B):
                if b >= 2:
                    sp.wait_ge(s_res, b - 1)
                sp.dma_start(ga[:, b % 2, :, :], acc_v[0][b]).then_inc(s_in[b % 2], 16)
                sp.dma_start(gb[:, b % 2, :, :], acc_v[1][b]).then_inc(s_in[b % 2], 16)
            for n in range(2):
                sp.wait_ge(s_out[n], 16 * B // 2)

        @block.gpsimd
        def _(pool):
            pool.memset(ident[:, :], 0.0).then_inc(s_cf, 1)
            pool.memset(pick[:, :], 0.0).then_inc(s_cf, 1)
            pool.memset(spread[:, :], 0.0).then_inc(s_cf, 1)
            pool.iota(count[:, N:N + CAP], pattern=[[1, CAP]], base=1, channel_multiplier=0,
                      allow_small_or_imprecise_dtypes=True).then_inc(s_cst, 1)
            for n in range(2):
                pool.wait_ge(s_cst, n + 1)
                pool.iota(ranks[HALF * n:HALF * n + HALF, :], pattern=[[1, HALF]], base=1 + HALF * n,
                          channel_multiplier=0, allow_small_or_imprecise_dtypes=True).then_inc(s_cst, 1)
            pool.wait_ge(s_cf, 3)
            pool.wait_ge(s_cst, 3)
            pool.affine_select(out=ident[:, :], in_=ident[:, :], compare_op=ALU.not_equal, fill=1.0, base=0,
                               pattern=[[-1, P]], channel_multiplier=1).then_inc(s_cst, 1)
            for n in range(2):
                pool.wait_ge(s_cst, n + 4)
                half = pick[HALF * n:HALF * n + HALF, :]
                pool.affine_select(out=half, in_=half, compare_op=ALU.not_equal, fill=1.0, base=0,
                                   pattern=[[-1, E]], channel_multiplier=1).then_inc(s_cst, 1)

            def gather(e, k):
                pool.wait_ge(s_gi, e + 1)
                pool.sem_inc(s_passed, 1)
                pool.indirect_dma_start(out=xe[:, k, :], out_offset=None, in_=table_d,
                                        in_offset=bass.IndirectOffsetOnAxis(ap=gidx[:, k:k + 1], axis=0))\
                    .then_inc(s_xe[k], 16)

            def add(e, k):
                n = k % 2
                pool.wait_ge(s_ys, e + 1)
                if not (isinstance(e, int) and e < 2):
                    pool.wait_ge(s_sc[n], e * 8 - 8 * n)
                pool.sem_inc(s_passed, 1)
                pool.indirect_dma_start(out=acc[n], out_offset=bass.IndirectOffsetOnAxis(ap=sidx[:, k:k + 1], axis=0),
                                        in_=ys[:, k % 4, :], in_offset=None, bounds_check=N + CAP - 1,
                                        oob_is_err=True, compute_op=ALU.add).then_inc(s_sc[n], 16)

            for k in range(LEAD):
                gather(k, k)
            for k in range(RING):
                gather(k + LEAD, (k + LEAD) % RING)
                add(k, k)
            with pool.Fori(RING, E - 2 * RING + 1, RING) as e:
                for k in range(RING):
                    gather(e + (k + LEAD), (k + LEAD) % RING)
                    add(e + k, k)
            for k in range(RING):
                if k + LEAD < RING:
                    gather(E - RING + k + LEAD, k + LEAD)
                add(E - RING + k, k)
            pool.wait_ge(s_sc[0], 16 * E // 2)
            pool.wait_ge(s_sc[1], 16 * E // 2)

        @block.vector
        def _(dve):
            dve.wait_ge(s_pk, 16)
            dve.wait_ge(s_cst, 6)
            dve.tensor_tensor_scan(count[:, 0:N], picked[:, :], picked[:, :], 0.0, ALU.add, ALU.max)\
               .then_inc(s_cnt, 1)
            dve.wait_ge(s_cnt, 1)
            for n in range(HALF // 8):
                dve.max_index(found[:, 8 * n:8 * n + 8], ranks[:, 8 * n:8 * n + 8], count[:, :]).then_inc(s_fnd, 1)
            dve.wait_ge(s_fnd, HALF // 8)
            for n in range(2):
                dve.tensor_copy(spread[HALF * n:HALF * n + HALF, HALF * n:HALF * n + HALF],
                                found[HALF * n:HALF * n + HALF, :]).then_inc(s_spr, 1)
            dve.wait_ge(s_idx_mm, 1)
            dve.tensor_scalar(src_idx[:, :], ps_idx[:, 0:E], float(N - 1), None, ALU.min).then_inc(s_idx, 1)
            dve.tensor_copy(dst_idx[:, :], ps_idx[:, 0:E]).then_inc(s_idx, 1)
            dve.wait_ge(s_idx, 2)

            def index(e, k):
                dve.tensor_copy(gidx[:, k:k + 1], src_idx[:, bass.ds(e, 1)]).then_inc(s_gi, 1)

            for k in range(LEAD):
                index(k, k)

            def hidden(e, n):
                dve.wait_ge(s_th, e + 1)
                dve.scalar_tensor_tensor(out=gated[:, n, :], in0=th[:, n, :], scalar=1.0,
                                         in1=ps_h[n][0:I, 0:CAP], op0=ALU.add, op1=ALU.mult).then_inc(s_ga, 1)
                dve.wait_ge(s_ga, e + 1)
                dve.tensor_tensor(hT[:, n, :], ps_h[n][0:I, CAP:2 * CAP], gated[:, n, :], ALU.mult)\
                   .then_inc(s_hT, 1)

            def weigh(e, k, first):
                n = k % 2
                dve.tensor_copy(wcol[:, n:n + 1], xe[:, k, bass.ds(e + C, 1)]).then_inc(s_wc, 1)
                if not first:
                    dve.wait_ge(s_sc[n], e * 8 - 8 * n - 16)
                dve.tensor_copy(sidx[:, k:k + 1], dst_idx[:, bass.ds(e, 1)]).then_inc(s_si, 1)
                dve.wait_ge(s_wc, e + 1)
                dve.wait_ge(s_y_mm, e + 1)
                dve.tensor_scalar(ys[:, k % 4, :], ps_y[n][:, 0:C], wcol[:, n:n + 1], 0.5, ALU.mult, ALU.mult)\
                   .then_inc(s_ys, 1)

            def step(e, k, first=False, more=True):
                if more:
                    index(e + LEAD, (k + LEAD) % RING)
                hidden(e, k % 2)
                weigh(e, k, first)

            for k in range(RING):
                step(k, k, first=k < 4)
            with dve.Fori(RING, E - 2 * RING + 1, RING) as e:
                for k in range(RING):
                    step(e + k, k)
            for k in range(RING):
                step(E - RING + k, k, more=k + LEAD < RING)
            for b in range(B):
                dve.wait_ge(s_in[b % 2], 32 * (b // 2 + 1))
                if b >= 2:
                    dve.wait_ge(s_out[b % 2], 16 * (b // 2))
                dve.tensor_tensor(res[:, b % 2, :, :], ga[:, b % 2, :, :], gb[:, b % 2, :, :], ALU.add)\
                   .then_inc(s_res, 1)

        @block.scalar
        def _(act):
            def step(e, n):
                act.wait_ge(s_xT_mm, e + 1)
                if not (isinstance(e, int) and e < 2):
                    act.wait_ge(s_h_mm, e - 1)
                act.activation(xeT[:, n, :, :].rearrange("p a t -> p (a t)"), ps_x[n][:, 0:2 * CAP],
                               ACT.Copy).then_inc(s_xT, 1)

            def squash(e, n):
                act.wait_ge(s_h_mm, e + 1)
                if not (isinstance(e, int) and e < 2):
                    act.wait_ge(s_ga, e - 1)
                act.activation(th[:, n, :], ps_h[n][0:I, 0:CAP], ACT.Tanh, scale=0.5).then_inc(s_th, 1)

            step(0, 0)
            for e in range(2):
                step(e + 1, (e + 1) % 2)
                squash(e, e)
            with act.Fori(2, E - 2, 2) as e:
                for n in range(2):
                    step(e + (n + 1), (n + 1) % 2)
                    squash(e + n, n)
            step(E - 1, 1)
            squash(E - 2, 0)
            squash(E - 1, 1)
            for b in range(B):
                act.wait_ge(s_res, b + 1)
                act.dma_start(out_v[b], res[:, b % 2, :, :]).then_inc(s_out[b % 2], 16)

        @block.tensor
        def _(pe):
            pe.wait_ge(s_cst, 6)
            pe.wait_ge(s_spr, 2)
            pe.matmul(ps_idx[:, 0:E], spread[:, :], pick[:, :], start=True, stop=True).then_inc(s_idx_mm, 1)

            def turn(e, k, waited):
                n = k % 2
                pe.wait_ge(s_xe[k], waited)
                if not (isinstance(e, int) and e < 2):
                    pe.wait_ge(s_xT, e - 1)
                rows = xe[:, k, 0:C].rearrange("p (m j) -> p j m", j=CC)
                for j in range(CC):
                    mm = pe.transpose(ps_x[n][:, CAP * j:CAP * j + CAP], rows[:, j, :], ident[:, :])
                mm.then_inc(s_xT_mm, 1)

            def gate_up(e, k, waited):
                n, w_at = k % 2, (k // GRP, k % GRP)
                if k % GRP == 0:
                    pe.wait_ge(s_w[k // GRP], waited)
                pe.wait_ge(s_xT, e + 1)
                if not (isinstance(e, int) and e < 2):
                    pe.wait_ge(s_hT, e - 1)
                for m, w in enumerate((wg, wu)):
                    for j in range(CC):
                        mm = pe.matmul(ps_h[n][0:I, CAP * m:CAP * m + CAP], w[:, w_at[0], w_at[1], I * j:I * j + I],
                                       xeT[:, n, j, :], start=(j == 0), stop=(j == CC - 1))
                mm.then_inc(s_h_mm, 1)

            def project(e, k):
                n = k % 2
                pe.wait_ge(s_hT, e + 1)
                if not (isinstance(e, int) and e < 2):
                    pe.wait_ge(s_ys, e - 1)
                pe.matmul(ps_y[n][:, 0:C], hT[:, n, :], wd[:, k // GRP, k % GRP, :], start=True, stop=True)\
                  .then_inc(s_y_mm, 1)

            turn(0, 0, 16)
            for e in range(RING):
                turn(e + 1, (e + 1) % RING, 16 if e + 1 < RING else 32)
                gate_up(e, e, 48)
                if e:
                    project(e - 1, e - 1)
            with pe.Fori(1, E // RING - 1) as r:
                e0 = r * RING
                for k in range(RING):
                    turn(e0 + (k + 1), (k + 1) % RING, r * 16 + (16 if k + 1 < RING else 32))
                    gate_up(e0 + k, k, r * 48 + 48)
                    project(e0 + (k - 1), (k - 1) % RING)
            for k in range(RING):
                e = E - RING + k
                if k + 1 < RING:
                    turn(e + 1, k + 1, 16 * (E // RING))
                gate_up(e, k, 48 * (E // RING))
                project(e - 1, (k - 1) % RING)
            project(E - 1, RING - 1)


def layer_kernel(nc, x, w_attn, w_proj, w_router, gate, up, down, out):
    parts_d = nc.dram_tensor("parts_d", [B, 3, 2 * C, T], BF16, kind="Internal").ap()
    acc = [nc.dram_tensor(f"acc{n}_d", [N + CAP, C], F32, kind="Internal").ap() for n in range(2)]
    table_d = nc.dram_tensor("table_d", [N, ROWW], F32, kind="Internal").ap()
    maskT_d = nc.dram_tensor("maskT_d", [B, P, T], BF16, kind="Internal").ap()
    attention(nc, x, w_attn, w_proj, w_router, parts_d, acc[0], acc[1], table_d, maskT_d)
    experts(nc, gate, up, down, acc, table_d, maskT_d, out)


_INS = ["L0_attn_x", "L0_attn_w_attn", "L0_attn_w_proj", "L0_ffn_router_weight", "L0_ffn_gate_proj",
        "L0_ffn_up_proj", "L0_ffn_down_proj"]
_OUTS = [((B, T, C), "float32")]


def kernel(**inputs):
    import numpy as _np
    import concourse.bacc as _bacc
    from concourse import mybir as _mybir
    from concourse.bass_utils import run_bass_kernel_spmd as _run

    nc = _bacc.Bacc("TRN2", target_bir_lowering=False, num_devices=1)
    arrays, args = {}, []
    for name in _INS:
        a = _np.ascontiguousarray(inputs[name])
        arrays[f"in_{name}_dram"] = a
        args.append(nc.dram_tensor(f"in_{name}_dram", a.shape, _mybir.dt.from_np(a.dtype), kind="ExternalInput").ap())
    for i, (shape, dtype) in enumerate(_OUTS):
        dt = _mybir.dt.from_np(_np.dtype(dtype))
        args.append(nc.dram_tensor(f"out_{i}_dram", shape, dt, kind="ExternalOutput").ap())
    layer_kernel(nc, *args)
    r = _run(nc, [arrays], core_ids=[0])
    got = tuple(r.results[0][f"out_{i}_dram"] for i in range(len(_OUTS)))
    return got[0]
```

```python
from contextlib import ExitStack

import concourse.bass as bass
from concourse import mybir

ALU = mybir.AluOpType
ACT = mybir.ActivationFunctionType
AX = mybir.AxisListType
F32 = mybir.dt.float32
BF16 = mybir.dt.bfloat16
I32 = mybir.dt.int32
U32 = mybir.dt.uint32

P = 128
B = 8
T = 512
C = 256
H = 16
D = 16
E = 64
I = 96
TOPK = 8
CAP = 128
N = B * T
TT = T // P
CC = C // P
GH = 4
NG = H // GH
ROWW = C + E
EPS = 1e-5
SCALE = 0.25
NEG = -1e30
RUNS = ((0, 0, 0, 3), (3, 0, 1, 2), (5, 0, 2, 1))
KROWS = D * 6
MROWS = KROWS + 3
PST = 16 * 12
STK = 16 * 2 * len(RUNS)
PAIRS = H // 2
LAG = PAIRS // 2
FILLS = (((0, 3, 0),), ((0, 2, 0), (0, 0, 384)), ((1, 3, 0),), ((1, 2, 0), (1, 0, 384)), ((0, 1, 0), (1, 1, 256)))
FP = len(FILLS)
NF = FP * PAIRS
MAXIMA = 4 * H
MBANKS = 3
ST_AT = {0: 0, 1: 512, 3: 896, 2: 1024}
HALF = CAP // 2
FINDS = HALF // 8
RANK_STEPS = 5 + FINDS
RANK_0 = 2
PW = 1280
KB_OF_PART = ((0, 3), (1, 2))


def due(eng, sem, per, b, k, apart=None):
    if isinstance(b, int):
        if per * b + k > 0:
            eng.wait_ge(sem, per * b + k)
        return
    eng.wait_ge(sem, b * per + k)
    if apart is not None:
        eng.sem_inc(apart, 1)


def before(n):
    return n - MBANKS if n >= MBANKS else max(m for m in range(NF) if m % MBANKS == n) - NF


def maxima_by(n):
    pair, f = divmod(n, len(FILLS))
    return 8 * pair + sum(len(x) for x in FILLS[:f + 1])


def attention(nc, x, w_attn, w_proj, w_router, parts_d, acc0, acc1, table_d, first):
    x_v = x.rearrange("b (t p) c -> b p t c", p=P)
    acc0_v = acc0[0:N, :].rearrange("(b t p) c -> b p t c", t=TT, p=P)
    acc1_v = acc1[0:N, :].rearrange("(b t p) c -> b p t c", t=TT, p=P)
    table_v = table_d.rearrange("(b t p) c -> b p t c", t=TT, p=P)
    with ExitStack() as ctx:
        def sb(name, shape, dt=F32):
            return ctx.enter_context(nc.sbuf_tensor(name, shape, dt))

        def sem(name):
            return ctx.enter_context(nc.semaphore(name))

        wqkv = sb("wqkv", [P, CC, 3 * C])
        wp = sb("wp", [P, CC, C])
        wr = sb("wr", [P, CC, E])
        ident = sb("ident", [P, P])
        identb = sb("identb", [P, P], BF16)
        causal = sb("causal", [P, T])
        minus_half = sb("minus_half", [P, 2 * TT])
        zeros = sb("zeros", [P, C])
        xa = sb("xa", [P, TT, C])
        xb = sb("xb", [P, TT, C])
        xn = sb("xn", [P, TT, C])
        xnT = sb("xnT", [P, CC, T])
        stats1 = sb("stats1", [P, TT, 6])
        mv1 = sb("mv1", [P, TT, 2])
        ve1 = sb("ve1", [P, TT])
        shift1 = sb("shift1", [P, TT])
        rstd1 = sb("rstd1", [P, TT])
        part = [sb(f"part{n}", [P, 4, T], BF16) for n in range(3)]
        rest = sb("rest", [P, 2, T])
        Qs = [sb(f"Qs{n}", [P, H, T], BF16) for n in range(2)]
        Ks = [sb(f"Ks{n}", [P, H, T], BF16) for n in range(2)]
        Va = [sb(f"Va{n}", [P, TT, H, 2 * D]) for n in range(2)]
        junk = sb("junk", [P, MBANKS * T], BF16)
        rowmax = sb("rowmax", [P, TT, H])
        nrest = sb("nrest", [P, TT, GH])
        nparts = sb("nparts", [P, TT, 3, GH], BF16)
        npT = sb("npT", [3 * GH, T], BF16)
        pT = sb("pT", [P, 2 * GH, PW])
        oT = sb("oT", [P, NG, T])
        rsum = sb("rsum", [P, TT, H])
        y = sb("y", [P, TT, C])
        yT = sb("yT", [P, CC, T])
        x2 = sb("x2", [P, TT, C])
        stats2 = sb("stats2", [P, TT, 6])
        mv2 = sb("mv2", [P, TT, 2])
        ve2 = sb("ve2", [P, TT])
        shift2 = sb("shift2", [P, TT])
        rstd2 = sb("rstd2", [P, TT])
        row = sb("row", [P, TT, ROWW])
        xn2T = sb("xn2T", [P, CC, T])
        logit = sb("logit", [P, TT, E])
        cut = sb("cut", [P, TT, E])
        top = sb("top", [P, TT, TOPK])
        nmax = sb("nmax", [P, TT])
        chosen = sb("chosen", [P, TT, 2, E], BF16)
        ex = sb("ex", [P, TT, E])
        wts = sb("wts", [P, TT, E])
        wsum = sb("wsum", [P, TT])
        winv = sb("winv", [P, TT])
        chosenT = sb("chosenT", [P, T], BF16)
        chosen_before = sb("chosen_before", [P, 1])
        count = sb("count", [P, T + HALF])
        far = sb("far", [P, 1])
        found = sb("found", [P, HALF], U32)
        moved = sb("moved", [P, HALF])
        ranks = count[:, T:T + HALF]

        ps_max = [ctx.enter_context(nc.psum_tensor(f"ps_max{n}", [P, T], F32)) for n in range(MBANKS)]
        ps_exp = [ctx.enter_context(nc.psum_tensor(f"ps_exp{n}", [P, T], F32)) for n in range(2)]
        ps_pv = ctx.enter_context(nc.psum_tensor("ps_pv", [P, T], F32))
        ps_jobs = [ctx.enter_context(nc.psum_tensor(f"ps_job{n}", [P, T], F32)) for n in range(2)]

        s_w = sem("weights_in")
        s_passed = sem("passed")
        s_zero = sem("zeros_ready")
        s_const = sem("consts_ready")
        s_id0 = sem("const_fill")
        s_ones = [sem(f"ones_ready{n}") for n in range(2)]
        s_vones = sem("v_ones_ready")
        s_acc = sem("accumulators_zeroed")
        s_xa = sem("xa_in")
        s_xb = sem("xb_in")
        s_st1 = sem("stats1_ready")
        s_mv1 = sem("mv1_ready")
        s_ve1 = sem("ve1_ready")
        s_rs1 = sem("rstd1_ready")
        s_sh1 = sem("shift1_ready")
        s_xn = sem("xn_ready")
        s_xnT_mm = sem("xnT_in_psum")
        s_xnT = sem("xnT_ready")
        s_qk_mm = sem("qk_in_psum")
        s_p1 = sem("part1_ready")
        s_rest = sem("rest_ready")
        s_p2 = sem("part2_ready")
        s_p3 = sem("part3_ready")
        s_pst = sem("parts_stored")
        s_stk = [sem(f"stacks_in{n}") for n in range(2)]
        s_v_mm = sem("v_in_psum")
        s_v = sem("v_ready")
        s_s = sem("scores_in_psum")
        s_max = sem("rowmax_ready")
        s_np = sem("negmax_steps")
        s_np_mm = sem("negmaxT_in_psum")
        s_npT = sem("negmaxT_ready")
        s_nrow = [sem(f"negmax_rows_in{g}") for g in range(NG)]
        s_sT = sem("scoresT_in_psum")
        s_exp = sem("exp_ready")
        s_msk = sem("probs_masked")
        s_pv = sem("pv_in_psum")
        s_oT = sem("oT_ready")
        s_o_mm = sem("o_in_psum")
        s_rsum = sem("rowsum_inverse_ready")
        s_y = sem("y_ready")
        s_yT_mm = sem("yT_in_psum")
        s_yT = sem("yT_ready")
        s_pr_mm = sem("proj_in_psum")
        s_x2 = sem("x2_ready")
        s_x2st = sem("x2_stored")
        s_st2 = sem("stats2_ready")
        s_mv2 = sem("mv2_ready")
        s_ve2 = sem("ve2_ready")
        s_rs2 = sem("rstd2_ready")
        s_sh2 = sem("shift2_ready")
        s_row = sem("xn2_ready")
        s_x2T_mm = sem("xn2T_in_psum")
        s_x2T = sem("xn2T_ready")
        s_lg_mm = sem("logits_in_psum")
        s_lg = sem("logits_ready")
        s_top = sem("topk_steps")
        s_ex = sem("router_exp_ready")
        s_rowst = sem("table_stored")
        s_ch_mm = sem("chosenT_in_psum")
        s_ch = sem("chosenT_ready")
        s_rk = sem("rank_steps")

        JOBS = [
            (0, 0, "yT", 0, -2), (0, 1, "yT", 1, -2), (0, 3, "proj", 0, -2), (0, 4, "npT", 3, -1),
            (1, 4, "proj", 1, -2), (1, 4, "xnT", 0, 1), (2, 2, "xnT", 1, 1), (2, 3, "npT", 0, 0),
            (2, 4, "qk", 0, 1), (3, 1, "qk", 1, 1), (3, 1, "qk", 2, 1), (3, 4, "qk", 3, 1),
            (5, 0, "npT", 1, 0), (5, 1, "x2T", 0, -2), (5, 4, "x2T", 1, -2), (5, 4, "o", 0, -1),
            (6, 3, "lg", 0, -2), (6, 4, "o", 1, -1), (7, 0, "npT", 2, 0), (7, 1, "v", 0, 1),
            (7, 1, "o", 2, -1), (7, 1, "o", 3, -1), (7, 4, "ch", 0, -2), (7, 4, "v", 1, 1),
        ]
        ACT_AT = {
            (0, 0): [("oT", 0, -1)], (0, 1): [("yT", 0, -2), ("yT", 1, -2)], (0, 4): [("npT", 3, -1)],
            (1, 1): [("norm1", 0, 1)], (1, 2): [("norm1", 1, 1)],
            (1, 4): [("norm1", 2, 1), ("oT", 1, -1), ("norm1", 3, 1)], (2, 0): [("xnT", 0, 1)],
            (2, 2): [("xnT", 1, 1), ("npT", 0, 0)], (2, 4): [("part1", 0, 1), ("part1", 1, 1)],
            (3, 1): [("part2", 0, 1), ("part1", 2, 1), ("part2", 1, 1)],
            (3, 4): [("part2", 2, 1), ("oT", 2, -1), ("part1", 3, 1)],
            (4, 0): [("norm2", 0, -2), ("part2", 3, 1)], (4, 1): [("norm2", 1, -2)],
            (4, 3): [("norm2", 2, -2)], (4, 4): [("npT", 1, 0)], (5, 1): [("norm2", 3, -2)],
            (5, 2): [("x2T", 0, -2), ("oT", 3, -1)], (6, 1): [("x2T", 1, -2)], (6, 2): [("lg", 0, -2)],
            (6, 4): [("npT", 2, 0), ("v", 0, 1)], (7, 1): [("ex", 0, -2)],
            (7, 4): [("v", 1, 1), ("ch", 0, -2)],
        }
        DVE_AT = {
            (0, 0): [("neg0", 3, -1), ("neg1", 3, -1), ("neg2", 3, -1)],
            (0, 1): [("stat1", 0, 1), ("stat1", 1, 1), ("stat1", 2, 1), ("stat1", 3, 1)],
            (0, 2): [("neg3", 3, -1), ("aggr1", 0, 1)], (0, 3): [("proj", 0, -2)], (1, 0): [("shift1", 0, 1)],
            (1, 1): [("count", 0, -3)],
            (1, 4): [("find", 0, -3), ("neg0", 0, 0), ("neg1", 0, 0), ("proj", 1, -2), ("neg2", 0, 0)],
            (2, 0): [("stat2", 0, -2), ("neg3", 0, 0)],
            (2, 1): [("stat2", 1, -2), ("stat2", 2, -2), ("stat2", 3, -2)],
            (2, 4): [("aggr2", 0, -2), ("qk", 0, 1)], (3, 1): [("qk", 1, 1)], (3, 2): [("qk", 2, 1)],
            (3, 4): [("shift2", 0, -2), ("find", 1, -3), ("qk", 3, 1), ("neg0", 1, 0)],
            (4, 0): [("neg1", 1, 0)], (4, 2): [("neg2", 1, 0)], (4, 3): [("neg3", 1, 0)],
            (5, 1): [("find", 2, -3)], (5, 3): [("find", 3, -3)], (5, 4): [("find", 4, -3), ("neg0", 2, 0)],
            (6, 0): [("find", 5, -3), ("neg1", 2, 0)], (6, 1): [("neg2", 2, 0)],
            (6, 2): [("o", 0, -1), ("neg3", 2, 0)], (6, 3): [("top8", 0, -2), ("o", 1, -1)],
            (6, 4): [("cut", 0, -2)], (7, 1): [("o", 2, -1), ("choose", 0, -2), ("o", 3, -1)],
            (7, 2): [("find", 6, -3), ("w0", 0, -2)],
            (7, 4): [("w1", 0, -2), ("w2", 0, -2), ("find", 7, -3), ("w3", 0, -2), ("keep", 0, -3)],
        }
        POOL_AT = {
            (0, 1): [("rstd1", 0, 1)], (2, 4): [("rstd2", 0, -2)], (3, 0): [("part3", 0, 1)],
            (3, 2): [("part3", 1, 1)], (3, 4): [("part3", 2, 1), ("part3", 3, 1)],
        }
        TAKEN = {"xnT": (s_xnT, 2), "qk": (s_rest, 4), "v": (s_v, 2), "npT": (s_npT, 4), "o": (s_y, 4),
                 "yT": (s_yT, 2), "proj": (s_x2, 2), "x2T": (s_x2T, 2), "lg": (s_lg, 1), "ch": (s_ch, 1)}

        BANK = {(name, k): n % 2 for n, (_, _, name, k, _) in enumerate(JOBS)}

        def there(rep, off):
            return 0 <= rep + off < B

        def expo(i, rep, p):
            if p < LAG:
                return (i - 1, (rep - 1) % 2, 2 * (p + LAG)) if there(rep, -1) else None
            return (i, rep % 2, 2 * (p - LAG)) if there(rep, 0) else None

        def walk(eng, body):
            for i in range(-1, 3):
                body(i, i)
            with eng.Fori(3, B - 2, 2) as i:
                body(i, 3)
                body(i + 1, 4)
            for i in range(B - 1, B + 3):
                body(i, i)

        block = ctx.enter_context(nc.Block())

        @block.sync
        def _(sp):
            def body(i, rep):
                on = lambda off: 0 <= rep + off < B

                def negmax_rows(b, par, g):
                    due(sp, s_npT, NG, b, g + 1)
                    for n in range(3):
                        sp.dma_start(Qs[par][KROWS + n:KROWS + n + 1, GH * g:GH * g + GH, :],
                                     npT[GH * n:GH * n + GH, :]).then_inc(s_nrow[g], 16)

                def store_parts(b, k):
                    due(sp, s_p3, 4, b, k + 1)
                    h0 = k // 2 * H // 2
                    for n in range(3):
                        slot = n if k % 2 == 0 else 2 - n
                        sp.dma_start(parts_d[b, k % 2, h0:h0 + H // 2, slot, :, :],
                                     part[n][:, k, :]).then_inc(s_pst, 16)

                def load_stacks(b, par, half, stored):
                    due(sp, s_pst, PST, b, stored, apart=s_passed)
                    h0 = half * H // 2
                    for n, q_slot, k_slot, blocks in RUNS:
                        for m, st, slot in ((1, Ks, k_slot), (0, Qs, q_slot)):
                            src = parts_d[b, m, h0:h0 + H // 2, slot:slot + blocks, :, :]
                            sp.dma_start(st[par][D * n:D * (n + blocks), h0:h0 + H // 2, :],
                                         src.rearrange("h n d t -> (n d) h t")).then_inc(s_stk[half], 16)

                if on(1) and not (isinstance(i, int) and i == 0):
                    due(sp, s_xn, TT, i, TT)
                    sp.dma_start(xa[:, :, :], x_v[i + 1]).then_inc(s_xa, 16)
                first_batch = isinstance(i, int) and i == -1
                if first_batch:
                    sp.wait_ge(s_xn, TT)
                    sp.dma_start(xa[:, :, :], x_v[1]).then_inc(s_xa, 16)
                if on(-2):
                    due(sp, s_x2, 2, i - 3, 2)
                    sp.dma_start(xb[:, :, :], x_v[i - 2]).then_inc(s_xb, 16)
                if on(-1):
                    negmax_rows(i - 1, (rep - 1) % 2, 3)
                if on(-3):
                    due(sp, s_top, 15, i - 3, 15)
                    sp.dma_start(table_v[i - 3], row[:, :, :]).then_inc(s_rowst, 16)
                if on(-2):
                    due(sp, s_x2, 2, i - 2, 2)
                    sp.dma_start(acc0_v[i - 2], x2[:, :, :]).then_inc(s_x2st, 16)
                if on(0):
                    negmax_rows(i, rep % 2, 0)
                for half in range(2):
                    if on(1):
                        store_parts(i + 1, 2 * half)
                        store_parts(i + 1, 2 * half + 1)
                        if first_batch:
                            load_stacks(i + 1, (rep + 1) % 2, half, PST // 2 * (half + 1))
                if on(0):
                    negmax_rows(i, rep % 2, 1)
                if on(1) and not first_batch:
                    for half in range(2):
                        if on(-1) and half == 0:
                            due(sp, s_sT, NF, i - 1, NF, apart=s_passed)
                        if on(0) and half == 1:
                            due(sp, s_s, NF, i, NF // 2 + 1, apart=s_passed)
                        load_stacks(i + 1, (rep + 1) % 2, half, PST)
                if on(0):
                    negmax_rows(i, rep % 2, 2)
                if isinstance(i, int) and i == 0:
                    sp.wait_ge(s_zero, 1)
                    for acc in (acc0, acc1):
                        sp.dma_start(acc[N:N + P, :], zeros[:, :]).then_inc(s_acc, 16)
                if on(0):
                    sp.dma_start(acc1_v[i], zeros[:, :].unsqueeze(1).to_broadcast([P, TT, C])).then_inc(s_acc, 16)

            walk(sp, body)
            sp.wait_ge(s_acc, 16 * (B + 2))
            sp.wait_ge(s_x2st, 16 * B)
            sp.wait_ge(s_rowst, 16 * B)

        @block.gpsimd
        def _(pool):
            pool.memset(zeros[:, :], 0.0).then_inc(s_zero, 1)
            pool.iota(far[:, :], pattern=[[0, 1]], base=N - T, channel_multiplier=0,
                      allow_small_or_imprecise_dtypes=True).then_inc(s_const, 1)
            pool.iota(ranks, pattern=[[1, HALF]], base=1, channel_multiplier=0,
                      allow_small_or_imprecise_dtypes=True).then_inc(s_const, 1)
            pool.wait_ge(s_const, 2)
            for half in (far[HALF:P, :], ranks[HALF:P, :]):
                pool.tensor_scalar(half, half, float(HALF), None, ALU.add).then_inc(s_const, 1)
            pool.wait_ge(s_const, 4)
            for m in (ident, identb, causal):
                pool.memset(m[:, :], 0.0).then_inc(s_id0, 1)
            pool.memset(minus_half[:, :], -0.5).then_inc(s_const, 1)
            pool.wait_ge(s_id0, 3)
            for m in (ident, identb):
                pool.affine_select(out=m[:, :], in_=m[:, :], compare_op=ALU.not_equal, fill=1.0, base=0,
                                   pattern=[[-1, P]], channel_multiplier=1).then_inc(s_const, 1)
            diag = causal[:, T - P:T]
            pool.affine_select(out=diag, in_=diag, compare_op=ALU.is_ge, fill=NEG, base=0,
                               pattern=[[-1, P]], channel_multiplier=1).then_inc(s_const, 1)
            for v in Va:
                pool.memset(v[:, :, :, D:2 * D], 1.0).then_inc(s_vones, 1)
            pool.wait_ge(s_const, 8)

            def rstd(s_mv, s_ve, s_rs, mv, ve, out, b):
                due(pool, s_mv, TT, b, TT, apart=s_passed)
                pool.tensor_scalar(ve[:, :], mv[:, :, 1], EPS, None, ALU.add).then_inc(s_ve, 1)
                due(pool, s_ve, 1, b, 1)
                pool.tensor_tensor(out[:, :], ve[:, :], minus_half[:, 0:TT], ALU.pow).then_inc(s_rs, 1)

            def body(i, rep):
                for p in range(PAIRS):
                    for f in range(FP):
                        if (e := expo(i, rep, p)) is not None:
                            b, _, h0 = e
                            n = FP * (h0 // 2) + f
                            if f == FP - 1:
                                at = h0 % (2 * GH)
                                diag, blocks = pT[:, at:at + 2, ST_AT[2]:ST_AT[2] + P], 2
                            else:
                                v = pT[:, (h0 + f // 2) % (2 * GH), :].rearrange("p (a n) -> p a n", n=P)
                                diag, blocks = (v[:, 0:1, :], 1) if f % 2 == 0 else (v[:, 4:8:3, :], 2)
                            due(pool, s_exp, NF, b, n + 1, apart=s_passed)
                            pool.affine_select(out=diag, in_=diag, compare_op=ALU.is_ge, fill=0.0, base=0,
                                               pattern=[[0, blocks], [1, P]], channel_multiplier=-1)\
                                .then_inc(s_msk, 1)
                        for name, k, off in POOL_AT.get((p, f), ()):
                            if not there(rep, off):
                                continue
                            b = i + off
                            if name == "rstd1":
                                due(pool, s_xn, TT, b, 0)
                                rstd(s_mv1, s_ve1, s_rs1, mv1, ve1, rstd1, b)
                            if name == "rstd2":
                                due(pool, s_row, TT, b, 0)
                                rstd(s_mv2, s_ve2, s_rs2, mv2, ve2, rstd2, b)
                            if name == "part3":
                                due(pool, s_pst, PST, b, 0)
                                due(pool, s_p2, 4, b, k + 1)
                                pool.tensor_tensor(part[2][:, k, :], rest[:, k % 2, :], part[1][:, k, :],
                                                   ALU.subtract).then_inc(s_p3, 1)
                if isinstance(i, int) and i == -1:
                    pool.wait_ge(s_p3, 4)
                    pool.memset(Ks[1][KROWS:P, :, :], 1.0).then_inc(s_ones[1], 1)
                    pool.wait_ge(s_ones[1], 1)

            walk(pool, body)

        @block.scalar
        def _(act):
            act.dma_start(wqkv[:, :, :], w_attn.rearrange("(a p) n -> p a n", p=P)).then_inc(s_w, 16)
            act.dma_start(wp[:, :, :], w_proj.rearrange("(a p) n -> p a n", p=P)).then_inc(s_w, 16)
            act.dma_start(wr[:, :, :], w_router.rearrange("(a p) n -> p a n", p=P)).then_inc(s_w, 16)
            act.wait_ge(s_vones, 2)

            def norm(out, src, shift, rstd, s_in, s_out, b, t):
                due(act, s_in, 1, b, 1)
                act.activation(out[:, t, 0:C], src[:, t, :], ACT.Identity, bias=shift[:, t:t + 1],
                               scale=rstd[:, t:t + 1]).then_inc(s_out, 1)

            def take(name, k, b, par):
                ps_job = ps_jobs[BANK.get(("qk" if name == "part1" else name, k), 0)]
                job_a = ps_job[:, :].rearrange("p (a t) -> p a t", a=CC)
                job_b = ps_job[:, :].bitcast(BF16)
                if name == "norm1":
                    due(act, s_xnT_mm, 2, b, 0)
                    norm(xn, xa, shift1, rstd1, s_sh1, s_xn, b, k)
                if name == "norm2":
                    due(act, s_rowst, 16, b, 0)
                    norm(row, x2, shift2, rstd2, s_sh2, s_row, b, k)
                if name == "oT":
                    due(act, s_o_mm, TT, b, 0)
                    due(act, s_pv, NG, b, k + 1)
                    act.activation(oT[:, k, :], ps_pv[:, :], ACT.Copy).then_inc(s_oT, 1)
                if name == "ex":
                    due(act, s_top, 15, b, 9)
                    for t in range(TT):
                        act.activation(ex[:, t, :], logit[:, t, :], ACT.Exp, bias=nmax[:, t:t + 1])\
                           .then_inc(s_ex, 1)
                if name == "lg":
                    due(act, s_top, 15, b, 0)
                    due(act, s_lg_mm, 1, b, 1)
                    act.activation(logit[:, :, :], ps_job[:, 0:TT * E].rearrange("p (t e) -> p t e", e=E),
                                   ACT.Copy).then_inc(s_lg, 1)
                if name == "xnT":
                    due(act, s_v_mm, 2, b, 0)
                    due(act, s_xnT_mm, 2, b, k + 1)
                    act.activation(xnT[:, :, 2 * P * k:2 * P * k + 2 * P], job_a, ACT.Copy).then_inc(s_xnT, 1)
                if name == "part1":
                    due(act, s_pst, PST, b, 0)
                    due(act, s_qk_mm, 4, b, k + 1)
                    act.activation(part[0][:, k, :], ps_job[:, :], ACT.Copy).then_inc(s_p1, 1)
                if name == "part2":
                    due(act, s_rest, 4, b, k + 1)
                    act.activation(part[1][:, k, :], rest[:, k % 2, :], ACT.Copy).then_inc(s_p2, 1)
                if name == "v":
                    due(act, s_pv, NG, b - 2, NG)
                    due(act, s_v_mm, 2, b, k + 1)
                    act.activation(Va[par][:, 2 * k:2 * k + 2, :, 0:D],
                                   ps_job[:, :].rearrange("p (t h d) -> p t h d", t=2, d=D),
                                   ACT.Copy).then_inc(s_v, 1)
                if name == "npT":
                    if k == 0:
                        due(act, s_nrow[NG - 1], 48, b, 0)
                    else:
                        due(act, s_nrow[k - 1], 48, b, 48)
                    due(act, s_np_mm, NG, b, k + 1)
                    act.activation(npT[:, :], job_b[0:3 * GH, 0:T], ACT.Copy).then_inc(s_npT, 1)
                if name == "yT":
                    due(act, s_pr_mm, 2, b, 0)
                    due(act, s_yT_mm, 2, b, k + 1)
                    act.activation(yT[:, :, 2 * P * k:2 * P * k + 2 * P], job_a, ACT.Copy).then_inc(s_yT, 1)
                if name == "x2T":
                    due(act, s_lg_mm, 1, b, 0)
                    due(act, s_x2T_mm, 2, b, k + 1)
                    act.activation(xn2T[:, :, 2 * P * k:2 * P * k + 2 * P], job_a, ACT.Copy).then_inc(s_x2T, 1)
                if name == "ch":
                    due(act, s_rk, RANK_STEPS, b - 1, RANK_0 + 1)
                    due(act, s_ch_mm, 1, b, 1)
                    act.activation(chosenT[:, :], job_b[:, 0:T], ACT.Copy).then_inc(s_ch, 1)

            def body(i, rep):
                for p in range(PAIRS):
                    for f in range(FP):
                        if (e := expo(i, rep, p)) is not None:
                            b, _, h0 = e
                            n = FP * (h0 // 2) + f
                            if f == 0:
                                due(act, s_pv, NG, b, h0 // GH - 1)
                            due(act, s_sT, NF, b, n + 1)
                            at = (h0 + f // 2) % (2 * GH)
                            if f == FP - 1:
                                at = h0 % (2 * GH)
                                dst = pT[:, at:at + 2, ST_AT[2]:PW]
                                src = ps_exp[n % 2][:, :].rearrange("p (h n) -> p h n", h=2)
                            else:
                                c = T * (f % 2)
                                dst, src = pT[:, at, c:c + T], ps_exp[n % 2][:, :]
                            act.activation(dst, src, ACT.Exp, scale=SCALE).then_inc(s_exp, 1)
                        for name, k, off in ACT_AT.get((p, f), ()):
                            if there(rep, off):
                                take(name, k, i + off, (rep + off) % 2)

            walk(act, body)

        @block.tensor
        def _(pe):
            pe.wait_ge(s_const, 8)
            pe.wait_ge(s_w, 48)
            pe.wait_ge(s_vones, 2)

            def turned(ps_job, src, k):
                for a in range(CC):
                    for t in range(2):
                        mm = pe.transpose(ps_job[:, P * (2 * a + t):P * (2 * a + t) + P],
                                          src[:, 2 * k + t, P * a:P * a + P], ident[:, :])
                return mm

            def job(name, k, b):
                ps_job = ps_jobs[BANK[name, k]]
                job_b = ps_job[:, :].bitcast(BF16)
                if name == "xnT":
                    due(pe, s_xn, TT, b, 2 * k + 2)
                    turned(ps_job, xn, k).then_inc(s_xnT_mm, 1)
                if name == "qk":
                    due(pe, s_xnT, 2, b, 2)
                    c = P * (2 * (k % 2) + k // 2)
                    for a in range(CC):
                        mm = pe.matmul(ps_job[:, :], wqkv[:, a, c:c + P], xnT[:, a, :],
                                       start=(a == 0), stop=(a == CC - 1))
                    mm.then_inc(s_qk_mm, 1)
                if name == "v":
                    for t in (2 * k, 2 * k + 1):
                        for a in range(CC):
                            mm = pe.matmul(ps_job[:, C * (t % 2):C * (t % 2) + C], xnT[:, a, P * t:P * t + P],
                                           wqkv[:, a, 2 * C:3 * C], start=(a == 0), stop=(a == CC - 1))
                    mm.then_inc(s_v_mm, 1)
                if name == "npT":
                    due(pe, s_np, 4 * NG, b, 4 * k + 4)
                    for t in range(TT):
                        mm = pe.transpose(job_b[0:3 * GH, P * t:P * t + P],
                                          nparts[:, t, :, :].rearrange("p n h -> p (n h)"), identb[:, :])
                    mm.then_inc(s_np_mm, 1)
                if name == "o":
                    due(pe, s_oT, NG, b, NG)
                    for g in range(NG):
                        mm = pe.transpose(ps_job[:, P * g:P * g + P], oT[:, g, P * k:P * k + P], ident[:, :])
                    mm.then_inc(s_o_mm, 1)
                if name == "yT":
                    due(pe, s_y, TT, b, 2 * k + 2)
                    turned(ps_job, y, k).then_inc(s_yT_mm, 1)
                if name == "proj":
                    due(pe, s_yT, 2, b, k + 1)
                    for t in (2 * k, 2 * k + 1):
                        for a in range(CC):
                            mm = pe.matmul(ps_job[:, C * (t % 2):C * (t % 2) + C], yT[:, a, P * t:P * t + P],
                                           wp[:, a, :], start=(a == 0), stop=(a == CC - 1))
                    mm.then_inc(s_pr_mm, 1)
                if name == "x2T":
                    due(pe, s_row, TT, b, 2 * k + 2)
                    turned(ps_job, row, k).then_inc(s_x2T_mm, 1)
                if name == "lg":
                    due(pe, s_x2T, 2, b, 2)
                    for t in range(TT):
                        for a in range(CC):
                            mm = pe.matmul(ps_job[:, E * t:E * t + E], xn2T[:, a, P * t:P * t + P], wr[:, a, :],
                                           start=(a == 0), stop=(a == CC - 1))
                    mm.then_inc(s_lg_mm, 1)
                if name == "ch":
                    due(pe, s_top, 15, b, 11)
                    for t in range(TT):
                        mm = pe.transpose(job_b[:, P * t:P * t + P],
                                          chosen[:, t, :, :].rearrange("p r e -> p (r e)"), identb[:, :])
                    mm.then_inc(s_ch_mm, 1)

            def body(i, rep):
                last = {BANK[j[2], j[3]]: (j, i - 1) for j in JOBS if there(rep - 1, j[4])}
                for p in range(PAIRS):
                    for f in range(FP):
                        if there(rep, 0):
                            if f == 0 and p % (PAIRS // 2) == 0:
                                due(pe, s_stk[p // (PAIRS // 2)], STK, i, STK)
                            max_fill(i, rep % 2, p, f)
                        if (e := expo(i, rep, p)) is not None:
                            exp_fill(*e, f)
                        for j in JOBS:
                            _, _, name, k, off = j
                            if j[0:2] != (p, f) or not there(rep, off):
                                continue
                            bank = BANK[name, k]
                            if bank in last:
                                (_, _, lname, lk, loff), li = last[bank]
                                taken, per = TAKEN[lname]
                                due(pe, taken, per, li + loff, lk + 1)
                            job(name, k, i + off)
                            last[bank] = (j, i)
                        if f in (1, 3):
                            off = 0 if p >= 6 else -1
                            if there(rep, off):
                                g = (p + 2) // 2 % NG
                                value_part(i + off, (rep + off) % 2, g, p % 2, f // 2)

            def max_fill(b, par, p, f):
                n = FP * p + f
                due(pe, s_max, MAXIMA, b, maxima_by(before(n)))
                for head, qb, at in FILLS[f]:
                    h, w = 2 * p + head, P * (qb + 1)
                    mm = pe.matmul(ps_max[n % MBANKS][:, at:at + w], Qs[par][0:KROWS, h, P * qb:P * qb + P],
                                   Ks[par][0:KROWS, h, 0:w], start=True, stop=True)
                mm.then_inc(s_s, 1)

            def exp_fill(b, par, h0, f):
                n = FP * (h0 // 2) + f
                if isinstance(b, int) and b == 0 and n == 0:
                    pe.wait_ge(s_ones[0], 1)
                    pe.wait_ge(s_ones[1], 1)
                if f == 0 and h0 % GH == 0:
                    due(pe, s_nrow[h0 // GH], 48, b, 48)
                due(pe, s_exp, NF, b, n - 1)
                for head, block, at in FILLS[f]:
                    h, kb = h0 + head, 3 - block
                    w = T - P * kb
                    mm = pe.matmul(ps_exp[n % 2][:, at:at + w], Ks[par][0:MROWS, h, P * kb:P * kb + P],
                                   Qs[par][0:MROWS, h, P * kb:T], start=True, stop=True)
                mm.then_inc(s_sT, 1)

            def value_part(b, par, g, step, half):
                kb = KB_OF_PART[step][half]
                if kb == 0:
                    if g == 0:
                        due(pe, s_v, 2, b, 2)
                    due(pe, s_oT, NG, b, g)
                    due(pe, s_msk, NF, b, 2 * FP * (g + 1))
                at = ST_AT[kb]
                for j in range(GH):
                    h = GH * g + j
                    mm = pe.matmul(ps_pv[32 * j:32 * j + 32, P * kb:T], Va[par][:, kb, h, :],
                                   pT[:, h % (2 * GH), at:at + T - P * kb], start=(kb == 0),
                                   stop=(step == 1 and half == 1))
                if step == 1 and half == 1:
                    mm.then_inc(s_pv, 1)

            walk(pe, body)

        @block.vector
        def _(dve):
            dve.memset(chosen_before[:, :], 0.0).then_inc(s_rk, 1)
            dve.memset(first[:, :], 4.0 * N).then_inc(s_rk, 1)

            dve.wait_ge(s_const, 8)

            def negmax(b, g, step):
                m = rowmax[:, :, GH * g:GH * g + GH]
                if step == 0:
                    due(dve, s_np_mm, NG, b, g)
                    due(dve, s_max, MAXIMA, b, 4 * GH * (g + 1))
                    dve.tensor_scalar(nparts[:, :, 0, :], m, -1.0, None, ALU.mult).then_inc(s_np, 1)
                    return
                due(dve, s_np, 4 * NG, b, 4 * g + step)
                if step == 1:
                    dve.scalar_tensor_tensor(out=nrest[:, :, :], in0=m, scalar=-1.0, in1=nparts[:, :, 0, :],
                                             op0=ALU.mult, op1=ALU.subtract).then_inc(s_np, 1)
                if step == 2:
                    dve.tensor_copy(nparts[:, :, 1, :], nrest[:, :, :]).then_inc(s_np, 1)
                if step == 3:
                    dve.tensor_tensor(nparts[:, :, 2, :], nrest[:, :, :], nparts[:, :, 1, :],
                                      ALU.subtract).then_inc(s_np, 1)

            def norm_step(name, k, b):
                one = name[-1] == "1"
                src, stats, mv, rstd, shift = (xa, stats1, mv1, rstd1, shift1) if one else \
                    (x2, stats2, mv2, rstd2, shift2)
                s_st, s_mv, s_rs, s_sh = (s_st1, s_mv1, s_rs1, s_sh1) if one else (s_st2, s_mv2, s_rs2, s_sh2)
                if name[:-1] == "stat":
                    if one:
                        due(dve, s_xa, 16, b, 16)
                    else:
                        due(dve, s_x2, 2, b, 2)
                    dve.bn_stats(stats[:, k, :], src[:, k, :]).then_inc(s_st, 1)
                if name[:-1] == "aggr":
                    due(dve, s_st, TT, b, TT, apart=s_passed)
                    for t in range(TT):
                        dve.bn_aggr(mv[:, t, :], stats[:, t, :]).then_inc(s_mv, 1)
                if name[:-1] == "shift":
                    due(dve, s_rs, 1, b, 1)
                    dve.scalar_tensor_tensor(out=shift[:, :], in0=mv[:, :, 0], scalar=-1.0, in1=rstd[:, :],
                                             op0=ALU.mult, op1=ALU.mult).then_inc(s_sh, 1)

            def take(name, k, b):
                ps_job = ps_jobs[BANK.get((name, k), 0)]
                if name == "qk":
                    due(dve, s_p3, 4, b, k - 1)
                    due(dve, s_p1, 4, b, k + 1)
                    dve.tensor_tensor(rest[:, k % 2, :], ps_job[:, :], part[0][:, k, :],
                                      ALU.subtract).then_inc(s_rest, 1)
                if name == "o":
                    due(dve, s_yT_mm, 2, b, 0)
                    due(dve, s_o_mm, TT, b, k + 1)
                    o = ps_job[:, :].rearrange("p (h n) -> p h n", n=2 * D)
                    dve.reciprocal(rsum[:, k, :], o[:, :, D]).then_inc(s_rsum, 1)
                    due(dve, s_rsum, TT, b, k + 1)
                    dve.tensor_tensor(y[:, k, :].rearrange("p (h d) -> p h d", d=D), o[:, :, 0:D],
                                      rsum[:, k, :].unsqueeze(2).to_broadcast([P, H, D]),
                                      ALU.mult).then_inc(s_y, 1)
                if name == "proj":
                    due(dve, s_xb, 16, b, 16)
                    due(dve, s_x2st, 16, b, 0)
                    due(dve, s_row, TT, b, 0)
                    due(dve, s_pr_mm, 2, b, k + 1)
                    dve.tensor_tensor(x2[:, 2 * k:2 * k + 2, :], ps_job[:, :].rearrange("p (t c) -> p t c", t=2),
                                      xb[:, 2 * k:2 * k + 2, :], ALU.add).then_inc(s_x2, 1)
                if name == "top8":
                    due(dve, s_lg, 1, b, 1, apart=s_passed)
                    for t in range(TT):
                        dve.max(top[:, t, :], logit[:, t, :]).then_inc(s_top, 1)
                if name == "cut":
                    due(dve, s_top, 15, b, 4, apart=s_passed)
                    for t in range(TT):
                        dve.match_replace(cut[:, t, :], top[:, t, :], logit[:, t, :], -3e38).then_inc(s_top, 1)
                    due(dve, s_ex, TT, b, 0)
                    dve.tensor_scalar(nmax[:, :], top[:, :, 0], -1.0, None, ALU.mult).then_inc(s_top, 1)
                if name == "choose":
                    due(dve, s_ch_mm, 1, b, 0)
                    due(dve, s_top, 15, b, 9)
                    for r in range(2):
                        dve.tensor_tensor(chosen[:, :, r, :], logit[:, :, :], cut[:, :, :],
                                          ALU.not_equal).then_inc(s_top, 1)
                if name == "w0":
                    due(dve, s_top, 15, b, 11)
                    due(dve, s_ex, TT, b, TT)
                    dve.tensor_tensor(wts[:, :, :], ex[:, :, :], chosen[:, :, 0, :], ALU.mult).then_inc(s_top, 1)
                if name == "w1":
                    due(dve, s_top, 15, b, 12)
                    dve.tensor_reduce(wsum[:, :], wts[:, :, :], AX.X, ALU.add).then_inc(s_top, 1)
                if name == "w2":
                    due(dve, s_top, 15, b, 13)
                    dve.reciprocal(winv[:, :], wsum[:, :]).then_inc(s_top, 1)
                if name == "w3":
                    due(dve, s_rowst, 16, b, 0)
                    due(dve, s_top, 15, b, 14)
                    dve.tensor_tensor(row[:, :, C:ROWW], wts[:, :, :],
                                      winv[:, :].unsqueeze(2).to_broadcast([P, TT, E]), ALU.mult).then_inc(s_top, 1)

            def rank(name, k, b):
                if name == "count":
                    due(dve, s_rk, RANK_STEPS, b, RANK_0)
                    due(dve, s_ch, 1, b, 1, apart=s_passed)
                    dve.tensor_tensor_scan(count[:, 0:T], chosenT[:, :], chosenT[:, :], chosen_before[:, 0:1],
                                           ALU.add, ALU.max).then_inc(s_rk, 1)
                if name == "find":
                    if k == 0:
                        due(dve, s_rk, RANK_STEPS, b, RANK_0 + 1, apart=s_passed)
                    dve.max_index(found[:, 8 * k:8 * k + 8], ranks[:, 8 * k:8 * k + 8], count[:, :]).then_inc(s_rk, 1)
                if name == "keep":
                    due(dve, s_rk, RANK_STEPS, b, RANK_0 + 1 + FINDS)
                    dve.tensor_copy(chosen_before[:, :], count[:, T - 1:T]).then_inc(s_rk, 1)
                    dve.tensor_scalar(moved[:, :], found[:, :], float(T), far[:, 0:1], ALU.is_ge, ALU.mult)\
                       .then_inc(s_rk, 1)
                    due(dve, s_rk, RANK_STEPS, b, RANK_0 + 3 + FINDS)
                    dve.tensor_tensor(moved[:, :], moved[:, :], found[:, :], ALU.add).then_inc(s_rk, 1)
                    due(dve, s_rk, RANK_STEPS, b, RANK_0 + 4 + FINDS)
                    dve.scalar_tensor_tensor(out=first[:, :], in0=first[:, :], scalar=-float(T), in1=moved[:, :],
                                             op0=ALU.add, op1=ALU.min).then_inc(s_rk, 1)

            def body(i, rep):
                for p in range(PAIRS):
                    for f in range(FP):
                        if there(rep, 0):
                            n = FP * p + f
                            due(dve, s_s, NF, i, n + 1, apart=s_passed)
                            for head, qb, at in FILLS[f]:
                                h, w, o = 2 * p + head, P * (qb + 1), T * (n % MBANKS) + at
                                dve.tensor_tensor_reduce(junk[:, o:o + w], ps_max[n % MBANKS][:, at:at + w],
                                                         causal[:, T - w:T], 1.0, 0.0, ALU.add, ALU.max,
                                                         rowmax[:, qb, h:h + 1]).then_inc(s_max, 1)
                        for name, k, off in DVE_AT.get((p, f), ()):
                            if not there(rep, off):
                                continue
                            if name[:3] == "neg":
                                negmax(i + off, k, int(name[3]))
                            elif name[:-1] in ("stat", "aggr", "shift"):
                                norm_step(name, k, i + off)
                            elif name in ("count", "find", "keep"):
                                rank(name, k, i + off)
                            else:
                                take(name, k, i + off)
                if isinstance(i, int) and i == -1:
                    dve.memset(Ks[0][KROWS:P, :, :], 1.0).then_inc(s_ones[0], 1)

            walk(dve, body)


def experts(nc, gate, up, down, acc, table_d, first, out):
    GRP = 4
    RING = 2 * GRP
    LEAD = 6
    with ExitStack() as ctx:
        def sb(name, shape, dt=F32):
            return ctx.enter_context(nc.sbuf_tensor(name, shape, dt))

        def sem(name):
            return ctx.enter_context(nc.semaphore(name))

        spread = sb("spread", [P, CAP])
        pick = sb("pick", [P, E])
        ident = sb("ident2", [P, P])
        src_idx = sb("src_idx", [P, E], I32)
        dst_idx = sb("dst_idx", [P, E], I32)
        gidx = sb("gidx", [P, RING], I32)
        sidx = sb("sidx", [P, RING], I32)
        wg = sb("wg", [P, 2, GRP, 2 * I])
        wu = sb("wu", [P, 2, GRP, 2 * I])
        wd = sb("wd", [I, 2, GRP, C])
        xe = sb("xe", [P, RING, ROWW])
        xeT = sb("xeT", [P, 2, CC, CAP])
        th = sb("th", [I, 2, CAP])
        gated = sb("gated", [I, 2, CAP])
        hT = sb("hT", [I, 2, CAP])
        wcol = sb("wcol", [P, 2])
        ys = sb("ys", [P, 4, C])
        ga = sb("ga", [P, 2, 4, C])
        gb = sb("gb", [P, 2, 4, C])
        res = sb("res", [P, 2, 4, C])

        ps_idx = ctx.enter_context(nc.psum_tensor("ps_idx", [P, 512], F32))
        ps_x = [ctx.enter_context(nc.psum_tensor(f"ps_x{n}", [P, 512], F32)) for n in range(2)]
        ps_h = [ctx.enter_context(nc.psum_tensor(f"ps_h{n}", [P, 512], F32)) for n in range(2)]
        ps_y = [ctx.enter_context(nc.psum_tensor(f"ps_y{n}", [P, 512], F32)) for n in range(2)]

        s_passed = sem("passed2")
        s_cst = sem("consts2_ready")
        s_cf = sem("const2_fill")
        s_spr = sem("spread_ready")
        s_idx_mm = sem("idx_in_psum")
        s_idx = sem("idx_ready")
        s_w = [sem(f"expert_weights_in{n}") for n in range(2)]
        s_gi = sem("gather_idx_ready")
        s_si = sem("scatter_idx_ready")
        s_xe = [sem(f"gathered{n}") for n in range(RING)]
        s_xT_mm = sem("xeT_in_psum")
        s_xT = sem("xeT_ready")
        s_h_mm = sem("gate_up_in_psum")
        s_th = sem("tanh_ready")
        s_ga = sem("gated_ready")
        s_hT = sem("hT_ready")
        s_y_mm = sem("expert_out_in_psum")
        s_wc = sem("weight_col_ready")
        s_ys = sem("weighted_out_ready")
        s_sc = [sem(f"added{n}") for n in range(2)]
        s_in = [sem(f"sums_in{n}") for n in range(2)]
        s_res = sem("result_ready")
        s_out = [sem(f"result_stored{n}") for n in range(2)]

        block = ctx.enter_context(nc.Block())

        gate_v = gate.rearrange("(q e) (p j) i -> q p e (j i)", e=GRP, j=CC)
        up_v = up.rearrange("(q e) (p j) i -> q p e (j i)", e=GRP, j=CC)
        down_v = down.rearrange("(q e) i c -> q i e c", e=GRP)
        acc_v = [a[0:N, :].rearrange("(b t p) c -> b p t c", t=4, p=P) for a in acc]
        out_v = out.rearrange("b (t p) c -> b p t c", p=P)

        @block.sync
        def _(sp):
            def load(q, n):
                sp.dma_start(wg[:, n, :, :], gate_v[q]).then_inc(s_w[n], 16)
                sp.dma_start(wu[:, n, :, :], up_v[q]).then_inc(s_w[n], 16)
                sp.dma_start(wd[:, n, :, :], down_v[q]).then_inc(s_w[n], 16)

            load(0, 0)
            load(1, 1)
            with sp.Fori(1, E // RING) as r:
                for n in range(2):
                    sp.wait_ge(s_y_mm, r * RING + (GRP * (n + 1) - RING))
                    load(r * 2 + n, n)
            for n, (buf, s_added) in enumerate(((ga, s_sc[0]), (gb, s_sc[1]))):
                sp.wait_ge(s_added, 16 * E // 2)
                for b in range(2):
                    sp.dma_start(buf[:, b, :, :], acc_v[n][b]).then_inc(s_in[b], 16)
            for b in range(2, B):
                sp.wait_ge(s_res, b - 1)
                sp.dma_start(ga[:, b % 2, :, :], acc_v[0][b]).then_inc(s_in[b % 2], 16)
                sp.dma_start(gb[:, b % 2, :, :], acc_v[1][b]).then_inc(s_in[b % 2], 16)
            for n in range(2):
                sp.wait_ge(s_out[n], 16 * B // 2)

        @block.gpsimd
        def _(pool):
            pool.memset(ident[:, :], 0.0).then_inc(s_cf, 1)
            pool.memset(pick[:, :], 0.0).then_inc(s_cf, 1)
            pool.memset(spread[:, :], 0.0).then_inc(s_cf, 1)
            pool.wait_ge(s_cf, 3)
            pool.affine_select(out=ident[:, :], in_=ident[:, :], compare_op=ALU.not_equal, fill=1.0, base=0,
                               pattern=[[-1, P]], channel_multiplier=1).then_inc(s_cst, 1)
            for n in range(2):
                pool.wait_ge(s_cst, n + 1)
                half = pick[HALF * n:HALF * n + HALF, :]
                pool.affine_select(out=half, in_=half, compare_op=ALU.not_equal, fill=1.0, base=0,
                                   pattern=[[-1, E]], channel_multiplier=1).then_inc(s_cst, 1)

            def gather(e, k):
                pool.wait_ge(s_gi, e + 1)
                pool.sem_inc(s_passed, 1)
                pool.indirect_dma_start(out=xe[:, k, :], out_offset=None, in_=table_d,
                                        in_offset=bass.IndirectOffsetOnAxis(ap=gidx[:, k:k + 1], axis=0))\
                    .then_inc(s_xe[k], 16)

            def add(e, k):
                n = k % 2
                pool.wait_ge(s_ys, e + 1)
                if not (isinstance(e, int) and e < 2):
                    pool.wait_ge(s_sc[n], e * 8 - 8 * n)
                pool.sem_inc(s_passed, 1)
                pool.indirect_dma_start(out=acc[n], out_offset=bass.IndirectOffsetOnAxis(ap=sidx[:, k:k + 1], axis=0),
                                        in_=ys[:, k % 4, :], in_offset=None, bounds_check=N + CAP - 1,
                                        oob_is_err=True, compute_op=ALU.add).then_inc(s_sc[n], 16)

            for k in range(LEAD):
                gather(k, k)
            for k in range(RING):
                gather(k + LEAD, (k + LEAD) % RING)
                add(k, k)
            with pool.Fori(RING, E - 2 * RING + 1, RING) as e:
                for k in range(RING):
                    gather(e + (k + LEAD), (k + LEAD) % RING)
                    add(e + k, k)
            for k in range(RING):
                if k + LEAD < RING:
                    gather(E - RING + k + LEAD, k + LEAD)
                add(E - RING + k, k)
            pool.wait_ge(s_sc[0], 16 * E // 2)
            pool.wait_ge(s_sc[1], 16 * E // 2)

        @block.vector
        def _(dve):
            dve.wait_ge(s_cst, 3)
            for n in range(2):
                dve.tensor_scalar(spread[HALF * n:HALF * n + HALF, HALF * n:HALF * n + HALF],
                                  first[HALF * n:HALF * n + HALF, :], float(N - T), None, ALU.add).then_inc(s_spr, 1)
            dve.wait_ge(s_idx_mm, 1)
            dve.tensor_scalar(src_idx[:, :], ps_idx[:, 0:E], float(N - 1), None, ALU.min).then_inc(s_idx, 1)
            dve.tensor_copy(dst_idx[:, :], ps_idx[:, 0:E]).then_inc(s_idx, 1)
            dve.wait_ge(s_idx, 2)

            def index(e, k):
                dve.tensor_copy(gidx[:, k:k + 1], src_idx[:, bass.ds(e, 1)]).then_inc(s_gi, 1)

            for k in range(LEAD):
                index(k, k)

            def hidden(e, n):
                dve.wait_ge(s_th, e + 1)
                dve.scalar_tensor_tensor(out=gated[:, n, :], in0=th[:, n, :], scalar=1.0,
                                         in1=ps_h[n][0:I, 0:CAP], op0=ALU.add, op1=ALU.mult).then_inc(s_ga, 1)
                dve.wait_ge(s_ga, e + 1)
                dve.tensor_tensor(hT[:, n, :], ps_h[n][0:I, CAP:2 * CAP], gated[:, n, :], ALU.mult)\
                   .then_inc(s_hT, 1)

            def weigh(e, k, first):
                n = k % 2
                dve.tensor_copy(wcol[:, n:n + 1], xe[:, k, bass.ds(e + C, 1)]).then_inc(s_wc, 1)
                if not first:
                    dve.wait_ge(s_sc[n], e * 8 - 8 * n - 16)
                dve.tensor_copy(sidx[:, k:k + 1], dst_idx[:, bass.ds(e, 1)]).then_inc(s_si, 1)
                dve.wait_ge(s_wc, e + 1)
                dve.wait_ge(s_si, e + 1)
                dve.wait_ge(s_y_mm, e + 1)
                dve.tensor_scalar(ys[:, k % 4, :], ps_y[n][:, 0:C], wcol[:, n:n + 1], 0.5, ALU.mult, ALU.mult)\
                   .then_inc(s_ys, 1)

            def step(e, k, first=False, more=True):
                if more:
                    index(e + LEAD, (k + LEAD) % RING)
                hidden(e, k % 2)
                weigh(e, k, first)

            for k in range(RING):
                step(k, k, first=k < 4)
            with dve.Fori(RING, E - 2 * RING + 1, RING) as e:
                for k in range(RING):
                    step(e + k, k)
            for k in range(RING):
                step(E - RING + k, k, more=k + LEAD < RING)
            for b in range(B):
                dve.wait_ge(s_in[b % 2], 32 * (b // 2 + 1))
                if b >= 2:
                    dve.wait_ge(s_out[b % 2], 16 * (b // 2))
                dve.tensor_tensor(res[:, b % 2, :, :], ga[:, b % 2, :, :], gb[:, b % 2, :, :], ALU.add)\
                   .then_inc(s_res, 1)

        @block.scalar
        def _(act):
            def step(e, n):
                act.wait_ge(s_xT_mm, e + 1)
                if not (isinstance(e, int) and e < 2):
                    act.wait_ge(s_h_mm, e - 1)
                act.activation(xeT[:, n, :, :].rearrange("p a t -> p (a t)"), ps_x[n][:, 0:2 * CAP],
                               ACT.Copy).then_inc(s_xT, 1)

            def squash(e, n):
                act.wait_ge(s_h_mm, e + 1)
                if not (isinstance(e, int) and e < 2):
                    act.wait_ge(s_ga, e - 1)
                act.activation(th[:, n, :], ps_h[n][0:I, 0:CAP], ACT.Tanh, scale=0.5).then_inc(s_th, 1)

            step(0, 0)
            for e in range(2):
                step(e + 1, (e + 1) % 2)
                squash(e, e)
            with act.Fori(2, E - 2, 2) as e:
                for n in range(2):
                    step(e + (n + 1), (n + 1) % 2)
                    squash(e + n, n)
            step(E - 1, 1)
            squash(E - 2, 0)
            squash(E - 1, 1)
            for b in range(B):
                act.wait_ge(s_res, b + 1)
                act.dma_start(out_v[b], res[:, b % 2, :, :]).then_inc(s_out[b % 2], 16)

        @block.tensor
        def _(pe):
            pe.wait_ge(s_cst, 3)
            pe.wait_ge(s_spr, 2)
            pe.matmul(ps_idx[:, 0:E], spread[:, :], pick[:, :], start=True, stop=True).then_inc(s_idx_mm, 1)

            def turn(e, k, waited):
                n = k % 2
                pe.wait_ge(s_xe[k], waited)
                if not (isinstance(e, int) and e < 2):
                    pe.wait_ge(s_xT, e - 1)
                rows = xe[:, k, 0:C].rearrange("p (m j) -> p j m", j=CC)
                for j in range(CC):
                    mm = pe.transpose(ps_x[n][:, CAP * j:CAP * j + CAP], rows[:, j, :], ident[:, :])
                mm.then_inc(s_xT_mm, 1)

            def gate_up(e, k, waited):
                n, w_at = k % 2, (k // GRP, k % GRP)
                if k % GRP == 0:
                    pe.wait_ge(s_w[k // GRP], waited)
                pe.wait_ge(s_xT, e + 1)
                if not (isinstance(e, int) and e < 2):
                    pe.wait_ge(s_hT, e - 1)
                for m, w in enumerate((wg, wu)):
                    for j in range(CC):
                        mm = pe.matmul(ps_h[n][0:I, CAP * m:CAP * m + CAP], w[:, w_at[0], w_at[1], I * j:I * j + I],
                                       xeT[:, n, j, :], start=(j == 0), stop=(j == CC - 1))
                mm.then_inc(s_h_mm, 1)

            def project(e, k):
                n = k % 2
                pe.wait_ge(s_hT, e + 1)
                if not (isinstance(e, int) and e < 2):
                    pe.wait_ge(s_ys, e - 1)
                pe.matmul(ps_y[n][:, 0:C], hT[:, n, :], wd[:, k // GRP, k % GRP, :], start=True, stop=True)\
                  .then_inc(s_y_mm, 1)

            turn(0, 0, 16)
            for e in range(RING):
                turn(e + 1, (e + 1) % RING, 16 if e + 1 < RING else 32)
                gate_up(e, e, 48)
                if e:
                    project(e - 1, e - 1)
            with pe.Fori(1, E // RING - 1) as r:
                e0 = r * RING
                for k in range(RING):
                    turn(e0 + (k + 1), (k + 1) % RING, r * 16 + (16 if k + 1 < RING else 32))
                    gate_up(e0 + k, k, r * 48 + 48)
                    project(e0 + (k - 1), (k - 1) % RING)
            for k in range(RING):
                e = E - RING + k
                if k + 1 < RING:
                    turn(e + 1, k + 1, 16 * (E // RING))
                gate_up(e, k, 48 * (E // RING))
                project(e - 1, (k - 1) % RING)
            project(E - 1, RING - 1)


def layer_kernel(nc, x, w_attn, w_proj, w_router, gate, up, down, out):
    parts_d = nc.dram_tensor("parts_d", [B, 2, H, 3, D, T], BF16, kind="Internal").ap()
    acc = [nc.dram_tensor(f"acc{n}_d", [N + CAP, C], F32, kind="Internal").ap() for n in range(2)]
    table_d = nc.dram_tensor("table_d", [N, ROWW], F32, kind="Internal").ap()
    with nc.sbuf_tensor("first_token", [P, HALF], F32) as first:
        attention(nc, x, w_attn, w_proj, w_router, parts_d, acc[0], acc[1], table_d, first)
        experts(nc, gate, up, down, acc, table_d, first, out)


_INS = ["L0_attn_x", "L0_attn_w_attn", "L0_attn_w_proj", "L0_ffn_router_weight", "L0_ffn_gate_proj",
        "L0_ffn_up_proj", "L0_ffn_down_proj"]
_OUTS = [((B, T, C), "float32")]


def kernel(**inputs):
    import numpy as _np
    import concourse.bacc as _bacc
    from concourse import mybir as _mybir
    from concourse.bass_utils import run_bass_kernel_spmd as _run

    nc = _bacc.Bacc("TRN2", target_bir_lowering=False, num_devices=1)
    arrays, args = {}, []
    for name in _INS:
        a = _np.ascontiguousarray(inputs[name])
        arrays[f"in_{name}_dram"] = a
        args.append(nc.dram_tensor(f"in_{name}_dram", a.shape, _mybir.dt.from_np(a.dtype), kind="ExternalInput").ap())
    for i, (shape, dtype) in enumerate(_OUTS):
        dt = _mybir.dt.from_np(_np.dtype(dtype))
        args.append(nc.dram_tensor(f"out_{i}_dram", shape, dt, kind="ExternalOutput").ap())
    layer_kernel(nc, *args)
    r = _run(nc, [arrays], core_ids=[0])
    got = tuple(r.results[0][f"out_{i}_dram"] for i in range(len(_OUTS)))
    return got[0]
```
